# Optimizing a Trainium2 kernel written in Bass

```python
import numpy as np
import jax
import jax.numpy as jnp

def _softmax(x, axis=-1):
    return jax.nn.softmax(x, axis=axis)

def _gelu(x):
    return jax.nn.gelu(x, approximate=True)

def _silu(x):
    return jax.nn.silu(x)

def _sigmoid(x):
    return jax.nn.sigmoid(x)

def _layernorm(x, axis=-1, eps=1e-05):
    m = jnp.mean(x, axis=axis, keepdims=True)
    v = jnp.var(x, axis=axis, keepdims=True)
    return (x - m) / jnp.sqrt(v + eps)

def _scatter_add(tgt, idx, src, axis=0):
    return tgt.at[idx].add(src)

def _segment_sum(src, seg, n):
    return jax.ops.segment_sum(src, seg, n)
kernel_name = 'mk_gnn_preln_d1_gnn_r64_530104'

def setup_inputs(seed: int=0):
    np.random.seed(seed)
    _w = jnp.asarray

    def _rec_inputs():
        import jax
        import jax.numpy as jnp
        _gk = jax.random.key(seed)
        x = -0.0001126 + 1 * jax.random.normal(jax.random.fold_in(_gk, 1), (10000, 768), jnp.float32)
        src = jax.random.randint(jax.random.fold_in(_gk, 2), (2500,), 0, 10000, jnp.int32)
        dst = jax.random.randint(jax.random.fold_in(_gk, 3), (2500,), 0, 10000, jnp.int32)
        _o = jnp.argsort(dst, stable=True)
        src = src[_o]
        dst = dst[_o]
        return (x, src, dst)
    x, src, dst = _rec_inputs()

    def _L0_gnn_setup():
        import jax, jax.numpy as jnp
        import numpy as np
        N = 10000
        E = 100000
        D = 768
        H = 1536
        EPS_MSG = 1e-07
        EPS_BN = 1e-05

        def segment_softmax(logits, seg, num_segments):
            m = jax.ops.segment_max(logits, seg, num_segments=num_segments)
            m = jnp.where(jnp.isfinite(m), m, 0.0)
            e = jnp.exp(logits - m[seg])
            s = jax.ops.segment_sum(e, seg, num_segments=num_segments)
            return e / (s[seg] + 1e-16)
        key = jax.random.key(seed)
        ks = jax.random.split(key, 8)
        x = jax.random.normal(ks[0], (N, D), dtype=jnp.float32)
        edge_index = jax.random.randint(ks[1], (2, E), 0, N, dtype=jnp.int32)
        batch = jnp.zeros((N,), dtype=jnp.int32)
        t = jnp.asarray(1.0, dtype=jnp.float32)
        s1 = 1.0 / np.sqrt(D)
        s2 = 1.0 / np.sqrt(H)
        W1 = jax.random.uniform(ks[2], (D, H), jnp.float32, -s1, s1)
        b1 = jax.random.uniform(ks[3], (H,), jnp.float32, -s1, s1)
        bn_gamma = jnp.ones((H,), jnp.float32)
        bn_beta = jnp.zeros((H,), jnp.float32)
        bn_mean = jnp.zeros((H,), jnp.float32)
        bn_var = jnp.ones((H,), jnp.float32)
        W2 = jax.random.uniform(ks[4], (H, D), jnp.float32, -s2, s2)
        b2 = jax.random.uniform(ks[5], (D,), jnp.float32, -s2, s2)
        return {'x': x, 'edge_index': edge_index, 'batch': batch, 't': t, 'W1': W1, 'b1': b1, 'bn_gamma': bn_gamma, 'bn_beta': bn_beta, 'bn_mean': bn_mean, 'bn_var': bn_var, 'W2': W2, 'b2': b2}
    _L0_gnn_all = _L0_gnn_setup()
    _L0_gnn_in = {k: v for k, v in _L0_gnn_all.items() if k in ('t', 'W1', 'b1', 'bn_gamma', 'bn_beta', 'bn_mean', 'bn_var', 'W2', 'b2')}
    del _L0_gnn_all
    return {'x': x, 'src': src, 'dst': dst, 'L0_gnn_t': _L0_gnn_in['t'], 'L0_gnn_W1': _L0_gnn_in['W1'], 'L0_gnn_b1': _L0_gnn_in['b1'], 'L0_gnn_bn_gamma': _L0_gnn_in['bn_gamma'], 'L0_gnn_bn_beta': _L0_gnn_in['bn_beta'], 'L0_gnn_bn_mean': _L0_gnn_in['bn_mean'], 'L0_gnn_bn_var': _L0_gnn_in['bn_var'], 'L0_gnn_W2': _L0_gnn_in['W2'], 'L0_gnn_b2': _L0_gnn_in['b2']}

def reference(x, src, dst, L0_gnn_t, L0_gnn_W1, L0_gnn_b1, L0_gnn_bn_gamma, L0_gnn_bn_beta, L0_gnn_bn_mean, L0_gnn_bn_var, L0_gnn_W2, L0_gnn_b2):
    import jax
    import jax.numpy as jnp

    def _L0_gnn_ref(x, edge_index, batch, t, W1, b1, bn_gamma, bn_beta, bn_mean, bn_var, W2, b2):
        import jax, jax.numpy as jnp
        import numpy as np
        N = 10000
        E = 100000
        D = 768
        H = 1536
        EPS_MSG = 1e-07
        EPS_BN = 1e-05

        def segment_softmax(logits, seg, num_segments):
            m = jax.ops.segment_max(logits, seg, num_segments=num_segments)
            m = jnp.where(jnp.isfinite(m), m, 0.0)
            e = jnp.exp(logits - m[seg])
            s = jax.ops.segment_sum(e, seg, num_segments=num_segments)
            return e / (s[seg] + 1e-16)
        src, dst = (edge_index[0], edge_index[1])
        msg = jax.nn.relu(x[src]) + EPS_MSG
        alpha = segment_softmax(msg * t, dst, N)
        agg = jax.ops.segment_sum(msg * alpha, dst, num_segments=N)
        out = agg + x
        z = out @ W1 + b1
        z = (z - bn_mean) * jax.lax.rsqrt(bn_var + EPS_BN) * bn_gamma + bn_beta
        z = jax.nn.relu(z)
        z = z @ W2 + b2
        return x + z
    edge_index = jnp.stack([src, dst])
    batch0 = jnp.zeros((10000,), jnp.int32)
    h = jnp.maximum(_layernorm(x, axis=-1), 0.0)
    x = x + _L0_gnn_ref(h, edge_index, batch0, L0_gnn_t, L0_gnn_W1, L0_gnn_b1, L0_gnn_bn_gamma, L0_gnn_bn_beta, L0_gnn_bn_mean, L0_gnn_bn_var, L0_gnn_W2, L0_gnn_b2)
    return x

_drawn_inputs = setup_inputs


def setup_inputs(seed=0):
    import zlib

    import numpy as np

    out = dict(_drawn_inputs(seed))
    spreads = {'L0_gnn_bn_gamma': (1.0, 0.6),
     'L0_gnn_bn_beta': (0.0, 0.326),
     'L0_gnn_bn_mean': (0.0, 0.305),
     'L0_gnn_bn_var': (1.0, 0.6)}
    factors = {'L0_gnn_b1': 8.0, 'L0_gnn_b2': 6.286}
    for name, (base, spread) in spreads.items():
        noise = np.random.default_rng([zlib.crc32(name.encode()), seed]).standard_normal(out[name].shape)
        drawn = base * np.exp(spread * noise) if base else spread * noise
        out[name] = jnp.asarray(drawn.astype(out[name].dtype))
    for name, factor in factors.items():
        out[name] = (out[name] * factor).astype(out[name].dtype)
    return out
```

```python
from contextlib import ExitStack

import concourse.bass as bass
from concourse import mybir


def gnn_layer(nc, x, src, dst, t_in, W1, b1, gamma, beta, mean, var, W2, b2, out):
    f32, f16, bf16, i32 = mybir.dt.float32, mybir.dt.float16, mybir.dt.bfloat16, mybir.dt.int32
    ALU = mybir.AluOpType
    ACT = mybir.ActivationFunctionType
    AX = mybir.AxisListType
    LARGEST = bass.bass_isa.ReduceOp.max

    P = 128
    N, D = x.shape
    E = src.shape[0]
    HID = W1.shape[1]
    KC, MC = D // P, HID // P
    R, T = 125, 4
    GW = R * T
    NG = N // GW
    NT = NG * T
    ET = E // R
    FREE_T = NT - ET
    EG = ET // T
    TAIL = FREE_T // T
    NJ = 80
    HALF = D // 2
    EPS_MSG, EPS_BN, EPS_LN, EPS_SUM = 1e-7, 1e-5, 1e-5, 1e-16
    XS = 512.0
    XMAX = 55.5
    NOWHERE = 20000
    EXP_BITS = 0x7F800000
    CONSTS = 14
    SCAN_STEPS = 10
    GROUP_EDGE0 = 2
    GROUP_SCAN0 = GROUP_EDGE0 + EG
    GROUP_PLAIN = GROUP_SCAN0 + KC
    assert NG * GW == N and ET * R == E and GROUP_PLAIN + 2 == TAIL and N < P * NJ

    agg_dram = nc.dram_tensor("agg_scratch", (KC, P, E), f32, kind="Internal").ap()

    ctx = ExitStack()
    with ctx:
        def sb(name, shape, dt):
            return ctx.enter_context(nc.sbuf_tensor(name, shape, dt))

        def sem(name):
            return ctx.enter_context(nc.semaphore(name))

        w1h, w1l = sb("w1h", [P, KC, HID], f16), sb("w1l", [P, KC, HID], f16)
        w2h, w2l = sb("w2h", [P, MC, D], f16), sb("w2l", [P, MC, D], f16)
        xin = sb("xin", [P, T, D], f32)
        base = sb("base", [P, T, D], f32)
        hrow = sb("hrow", [P, T, D], f32)
        xth, xtl = sb("xth", [P, KC, GW], f16), sb("xtl", [P, KC, GW], f16)
        ah, al = sb("ah", [P, MC, 512], f16), sb("al", [P, MC, 512], f16)
        b2row = sb("b2row", [P, D], f32)
        xsum = sb("xsum", [P, 2, GW], f32)
        arena = sb("arena", [P, 11256], f32)
        s0, s1, s2 = (arena[:, E * i:E * (i + 1)] for i in range(3))
        mark = [arena[:, 7500 + 1252 * i:7500 + 1252 * (i + 1)].bitcast(bf16) for i in range(3)]
        first, keep, cut = mark

        ident = sb("ident", [P, P], f32)
        ones = sb("ones", [P, P], f32)
        ones16 = sb("ones16", [P, P], bf16)
        before = sb("before", [P, P], f32)
        tie = sb("tie", [P, P], f32)
        lane = sb("lane", [P, P], f32)
        node = sb("node", [P, NJ], f32)
        part1 = sb("part1", [P, 1], f32)
        perm_f = sb("perm_f", [P, NJ], f32)
        perm_g = sb("perm_g", [P, NT], i32)
        perm_s = sb("perm_s", [P, NT], i32)
        src_g = sb("src_g", [P, ET], i32)
        idx_g, idx_s, idx_e = sb("idx_g", [P, T], i32), sb("idx_s", [P, T], i32), sb("idx_e", [P, T], i32)
        edge_i = sb("edge_i", [P, 4, ET], i32)
        edge_f = sb("edge_f", [P, 4, ET], f32)
        tab = sb("tab", [P, 8, NJ], f32)
        tab_i = sb("tab_i", [P, NJ], i32)
        count3 = sb("count3", [P, 3, ET], f32)
        sorted_e = sb("sorted_e", [P, 2, ET], f32)
        vecs = sb("vecs", [MC, 5, P], f32)
        vcol = sb("vcol", [P, 16, MC], f32)
        pcol = sb("pcol", [P, 2, MC], f32)
        scol = sb("scol", [P, 8], f32)
        tcol = sb("tcol", [P, 1], f32)
        bnraw, bnraw_e = sb("bnraw", [P, T, 12], f32), sb("bnraw_e", [P, T, 12], f32)
        mv, mv_e = sb("mv", [P, T, 2], f32), sb("mv_e", [P, T, 2], f32)
        ln, ln_e = sb("ln", [P, T, 3], f32), sb("ln_e", [P, T, 3], f32)
        neghalf = sb("neghalf", [P, MC], f32)

        wst1 = arena[:, 0:KC * HID].rearrange("p (c n) -> p c n", c=KC)
        wst2 = arena[:, 0:MC * D].rearrange("p (m n) -> p m n", m=MC)
        base_flat = base[:, :, :].rearrange("p t n -> p (t n)")
        w1abs = base_flat[:, 0:HID].bitcast(bf16).rearrange("p (s n) -> p s n", s=2)
        s1row = base_flat[:, HID:2 * HID]
        ah_flat = ah[:, :, :].rearrange("p m n -> p (m n)")
        al_flat = al[:, :, :].rearrange("p m n -> p (m n)")
        hot_p = ah_flat[:, 0:ET * P].bitcast(bf16).rearrange("p (j b) -> p j b", b=P)
        hot_j = ah_flat[:, ET * P:ET * (P + NJ)].bitcast(bf16).rearrange("p (j b) -> p j b", b=NJ)
        BJ = 10
        ring_b = ah_flat[:, 0:4 * BJ * R].bitcast(f32).rearrange("p (s j b) -> p s j b", s=2, j=BJ)
        ring_a = al_flat[:, 0:4 * BJ * NJ].bitcast(f32).rearrange("p (s j b) -> p s j b", s=2, j=BJ)
        dst_cols = s1[0:R, :].rearrange("p (j q) -> p j q", j=ET)
        dst_tied = s2[0:R, :].rearrange("p (j q) -> p j q", j=ET)
        slot_hot = s2[0:R, :].rearrange("p (j b) -> p j b", j=ET)
        tile_hot = s0[0:R, 0:2 * ET * ET].rearrange("p (j s a) -> p j s a", j=ET, s=2)
        tile_eq = s0[0:R, 1000:1000 + ET * ET].rearrange("p (j a) -> p j a", j=ET)
        dst_diag = s1[0:R, :].rearrange("p (a b) -> p a b", a=ET)
        picks = s1[0:R, 0:440]
        xedge = arena[:, 0:T * D].rearrange("p (t n) -> p t n", t=T)
        emsg = arena[:, T * D:T * D + 2 * GW].rearrange("p (s n) -> p s n", s=2)
        agg_in = arena[:, 0:KC * GW].rearrange("p (c n) -> p c n", c=KC)

        def pb(name, shape, dt):
            return ctx.enter_context(nc.psum_tensor(name, shape, dt))

        ps1 = [pb(f"ps1_{i}", [P, 512], f32) for i in range(2)]
        pst = [pb(f"pst_{i}", [P, 512], f32) for i in range(2)]
        ps2 = [pb(f"ps2_{i}", [P, 2, 512], f32) for i in range(2)]

        in_edges, in_dstrow, in_vecs, in_b2, in_t = map(sem, ("in_edges", "in_dstrow", "in_vecs", "in_b2", "in_t"))
        in_w1 = [sem(f"in_w1_{c}") for c in range(KC)]
        in_w2 = [sem(f"in_w2_{q}") for q in range(3)]
        const_done = sem("const_done")
        dve_step = sem("dve_step")
        pool_turn = sem("pool_turn")
        dve_turn = sem("dve_turn")
        hot_ready, hot_used = sem("hot_ready"), sem("hot_used")
        count_done, offset_done, perm_done = sem("count_done"), sem("offset_done"), sem("perm_done")
        rowtot_ready = sem("rowtot_ready")
        perm_ready, pads_zero = sem("perm_ready"), sem("pads_zero")
        abs_ready, abs_used, norm_done = sem("abs_ready"), sem("abs_used"), sem("norm_done")
        s1_ready, w1s_dve, w1s_pool = sem("s1_ready"), sem("w1s_dve"), sem("w1s_pool")
        w1h_ready, w1l_ready = sem("w1h_ready"), sem("w1l_ready")
        vecs_done, s1col_done = sem("vecs_done"), sem("s1col_done")
        varp_ready, pow_ready, bn_ready = sem("varp_ready"), sem("pow_ready"), sem("bn_ready")
        w2max_ready, w2max_all, w2scale_ready = sem("w2max_ready"), sem("w2max_all"), sem("w2scale_ready")
        w2h_ready, w2l_ready = sem("w2h_ready"), sem("w2l_ready")
        sort_hot, sorted_done = sem("sort_hot"), sem("sorted_done")
        diag_ready, row_done, row_used = sem("diag_ready"), sem("row_done"), sem("row_used")
        pick_hot, picks_done = sem("pick_hot"), sem("picks_done")
        picks_copied = sem("picks_copied")
        rows_in = [sem(f"rows_in_{t}") for t in range(T)]
        rows_out = [sem(f"rows_out_{t}") for t in range(T)]
        idx_ready, bn_raw, mv_ready, ln_step = sem("idx_ready"), sem("bn_raw"), sem("mv_ready"), sem("ln_step")
        h_ready, res_ready, base_ready = sem("h_ready"), sem("res_ready"), sem("base_ready")
        tr_done, sum_done, xh_ready, xl_ready = sem("tr_done"), sem("sum_done"), sem("xh_ready"), sem("xl_ready")
        mm1_done, act_done, ah_ready, al_ready = sem("mm1_done"), sem("act_done"), sem("ah_ready"), sem("al_ready")
        mm2_done, fin_ready = sem("mm2_done"), sem("fin_ready")
        e_idx_ready = sem("e_idx_ready")
        e_rows_in = [sem(f"e_rows_in_{t}") for t in range(T)]
        e_bn_raw, e_mv_ready, e_ln_step, e_h_ready = map(sem, ("e_bn_raw", "e_mv_ready", "e_ln_step", "e_h_ready"))
        e_tr_done, e_msg_ready = sem("e_tr_done"), sem("e_msg_ready")
        e_msg_out = [sem(f"e_msg_out_{i}") for i in range(2)]
        msg_in, scan_step, scan_act, agg_out, agg_back = map(sem, ("msg_in", "scan_step", "scan_act", "agg_out", "agg_back"))

        def wait(eng, s, v):
            if not (isinstance(v, int) and v <= 0):
                eng.wait_ge(s, v)

        def wait_turn(eng, s, v, turn):
            if isinstance(v, int):
                wait(eng, s, v)
            else:
                eng.wait_ge(s, v)
                eng.sem_inc(turn, 1)

        def spread(ap, shape, axis):
            return ap.unsqueeze(axis).to_broadcast(shape)

        block = ctx.enter_context(nc.Block())

        @block.sync
        def _(sp):
            sp.dma_start(edge_i[0:R, 1, :], dst.rearrange("(p j) -> p j", j=ET)).then_inc(in_edges, 16)
            sp.dma_start(edge_i[0:R, 0, :], src.rearrange("(p j) -> p j", j=ET)).then_inc(in_edges, 16)
            for c in range(KC):
                sp.dma_start(wst1[:, c, :], W1[P * c:P * (c + 1), :]).then_inc(in_w1[c], 16)
                if c == 1:
                    for i, v in enumerate((b1, gamma, beta, mean, var)):
                        sp.dma_start(vecs[:, i, :], v.rearrange("(m p) -> m p", p=P)).then_inc(in_vecs, 16)
            sp.dma_start(b2row[:, :], b2.partition_broadcast(P)).then_inc(in_b2, 16)
            sp.dma_start(tcol[:, :], t_in.partition_broadcast(P)).then_inc(in_t, 16)
            sp.wait_ge(w1l_ready, KC)
            for q in range(3):
                sp.dma_start(wst2[:, 4 * q:4 * q + 4, :],
                             W2[512 * q:512 * (q + 1), :].rearrange("(m p) n -> p m n", p=P)).then_inc(in_w2[q], 16)
            sp.wait_ge(w2l_ready, MC)
            sp.dma_start(s0[0:R, :].bitcast(i32), dst.partition_broadcast(R)).then_inc(in_dstrow, 16)

            def edge_group_out(e):
                for c in range(KC):
                    wait(sp, e_msg_ready, KC * e + c + 1)
                    sp.dma_start(agg_dram[c, :, bass.ds(GW * e, GW)], emsg[:, c % 2, :]).then_inc(e_msg_out[c % 2], 16)

            edge_group_out(0)
            with sp.Fori(1, EG) as e:
                edge_group_out(e)
            for i in range(2):
                sp.wait_ge(e_msg_out[i], 16 * EG * KC // 2)

            def scan_io(c):
                wait(sp, agg_out, 16 * c)
                sp.dma_start(s0, agg_dram[bass.ds(c, 1), :, :].rearrange("o p e -> (o p) e")).then_inc(msg_in, 16)
                wait(sp, scan_step, SCAN_STEPS * (c + 1))
                sp.dma_start(agg_dram[bass.ds(c, 1), :, :].rearrange("o p e -> (o p) e"), s1).then_inc(agg_out, 16)

            scan_io(0)
            with sp.Fori(1, KC) as c:
                scan_io(c)
            sp.wait_ge(agg_out, 16 * KC)

            def tail_group_in(e):
                wait(sp, sum_done, KC * e)
                sp.dma_start(agg_in, agg_dram[:, :, bass.ds(GW * e, GW)].rearrange("c p e -> p c e")).then_inc(agg_back, 16)

            tail_group_in(0)
            with sp.Fori(1, EG) as e:
                tail_group_in(e)

        @block.gpsimd
        def _(pool):
            bound = pool.to_reg(N - 1)

            def const(ins, steps=[0]):
                steps[0] += 1
                ins.then_inc(const_done, 1)
                return steps[0]

            const(pool.iota(lane[:, :], pattern=[[1, P]], base=0, channel_multiplier=0, allow_small_or_imprecise_dtypes=True))
            const(pool.iota(node[:, :], pattern=[[P, NJ]], base=0, channel_multiplier=1, allow_small_or_imprecise_dtypes=True))
            const(pool.memset(ones[:, :], 1.0))
            const(pool.iota(part1[:, :], pattern=[[1, 1]], base=1, channel_multiplier=1, allow_small_or_imprecise_dtypes=True))
            const(pool.memset(tie[:, :], -0.5))
            const(pool.memset(ident[:, :], 0.0))
            const(pool.memset(neghalf[:, :], -0.5))
            n = const(pool.memset(ones16[:, :], 1.0))
            pool.wait_ge(const_done, n)
            const(pool.affine_select(out=before[:, :], in_=ones[:, :], compare_op=ALU.is_gt, fill=0.0,
                                     base=0, pattern=[[1, P]], channel_multiplier=-1))
            const(pool.affine_select(out=tie[:, :], in_=tie[:, :], compare_op=ALU.is_gt, fill=0.0,
                                     base=0, pattern=[[-1, P]], channel_multiplier=1))
            const(pool.affine_select(out=ident[:, :], in_=ident[:, :], compare_op=ALU.not_equal, fill=1.0,
                                     base=0, pattern=[[-1, P]], channel_multiplier=1))
            const(pool.memset(perm_g[:, :], 0))
            const(pool.memset(src_g[:, :], 0))
            n = const(pool.memset(perm_s[:, :], NOWHERE))
            assert n == CONSTS

            def gather(q, t, index):
                pool.indirect_dma_start(xin[:, t, :], None, x, bass.IndirectOffsetOnAxis(ap=index, axis=0),
                                        bounds_check=bound, oob_is_err=False).then_inc(rows_in[t], 16)

            def norm_tile(q, t, m, l, s_mv, s_step):
                at = 4 * (T * q + t)
                wait_turn(pool, s_mv, T * q + t + 1, pool_turn)
                pool.tensor_scalar(l[:, t, 2:3], m[:, t, 1:2], EPS_LN, None, ALU.add).then_inc(s_step, 1)
                wait_turn(pool, s_step, at + 1, pool_turn)
                pool.tensor_tensor(l[:, t, 0:1], l[:, t, 2:3], neghalf[:, 0:1], ALU.pow).then_inc(s_step, 1)
                wait_turn(pool, s_step, at + 2, pool_turn)
                pool.tensor_tensor(l[:, t, 2:3], m[:, t, 0:1], l[:, t, 0:1], ALU.mult).then_inc(s_step, 1)
                wait_turn(pool, s_step, at + 3, pool_turn)
                pool.tensor_scalar(l[:, t, 1:2], l[:, t, 2:3], -1.0, None, ALU.mult).then_inc(s_step, 1)

            def residual(q, t):
                wait_turn(pool, h_ready, T * q + t + 1, pool_turn)
                pool.tensor_tensor(xin[:, t, :], xin[:, t, :], hrow[:, t, :], ALU.add).then_inc(res_ready, 1)

            def keep_base(q, t):
                wait_turn(pool, res_ready, T * q + t + 1, pool_turn)
                pool.tensor_tensor(base[:, t, :], xin[:, t, :], b2row[:, :], ALU.add).then_inc(base_ready, 1)

            def largest_w2():
                pool.wait_ge(w2max_ready, 1)
                pool.partition_all_reduce(scol[:, 1:2], scol[:, 0:1], P, LARGEST).then_inc(w2max_all, 1)

            def rows_next(q, beside=None):
                for t in range(T):
                    if beside and t == T - 1:
                        beside()
                    norm_tile(q, t, mv, ln, mv_ready, ln_step)
                    if t >= 1:
                        residual(q, t - 1)
                residual(q, T - 1)

            def indices(g):
                pool.tensor_copy(idx_s[:, :], perm_s[:, bass.ds(T * g, T)]).then_inc(idx_ready, 1)
                pool.tensor_copy(idx_g[:, :], perm_g[:, bass.ds(T * (g + 2), T)]).then_inc(idx_ready, 1)
                wait_turn(pool, idx_ready, 2 * g + 2, pool_turn)

            def rows_move(g, more):
                for t in range(T):
                    wait_turn(pool, fin_ready, T * g + t + 1, pool_turn)
                    pool.indirect_dma_start(out, bass.IndirectOffsetOnAxis(ap=idx_s[:, t:t + 1], axis=0), base[:, t, :],
                                            None, bounds_check=bound, oob_is_err=False).then_inc(rows_out[t], 16)
                    if more >= 1:
                        wait_turn(pool, rows_out[t], 16 * (g + 1), pool_turn)
                        keep_base(g + 1, t)
                    if more >= 2:
                        wait_turn(pool, base_ready, T * (g + 1) + t + 1, pool_turn)
                        gather(g + 2, t, idx_g[:, t:t + 1])

            pool.wait_ge(perm_ready, 1)
            for t in range(T):
                gather(0, t, perm_g[:, t:t + 1])
            pool.wait_ge(hot_used, NJ // BJ)
            pool.memset(ah[:, :, GW:512], 0.0).then_inc(pads_zero, 1)
            pool.memset(al[:, :, GW:512], 0.0).then_inc(pads_zero, 1)
            pool.wait_ge(s1_ready, 1)
            for c in range(4, KC):
                pool.wait_ge(in_w1[c], 16)
                pool.tensor_tensor(wst1[:, c, :], wst1[:, c, :], s1row, ALU.mult).then_inc(w1s_pool, 1)
            pool.wait_ge(varp_ready, 1)
            pool.tensor_tensor(vcol[:, 6, :], vcol[:, 5, :], neghalf[:, :], ALU.pow).then_inc(pow_ready, 1)
            rows_next(0)
            pool.wait_ge(w1s_dve, 4)
            pool.wait_ge(w1s_pool, 2)
            pool.wait_ge(s1col_done, 1)
            pool.wait_ge(in_b2, 16)
            for t in range(T):
                keep_base(0, t)
                pool.wait_ge(base_ready, t + 1)
                gather(1, t, perm_g[:, T + t:T + t + 1])

            rows_next(1, largest_w2)
            indices(0)
            rows_move(0, 2)
            rows_next(2)
            indices(1)
            rows_move(1, 2)

            pool.wait_ge(perm_ready, 2)

            def edge_group(e):
                g = e + GROUP_EDGE0
                pool.tensor_copy(idx_e[:, :], src_g[:, bass.ds(T * e, T)]).then_inc(e_idx_ready, 1)
                wait_turn(pool, e_idx_ready, e + 1, pool_turn)
                wait_turn(pool, e_tr_done, KC * e, pool_turn)
                for t in range(T):
                    pool.indirect_dma_start(xedge[:, t, :], None, x, bass.IndirectOffsetOnAxis(ap=idx_e[:, t:t + 1], axis=0),
                                            bounds_check=bound, oob_is_err=False).then_inc(e_rows_in[t], 16)
                rows_next(g + 1)
                indices(g)
                for t in range(T):
                    norm_tile(e, t, mv_e, ln_e, e_mv_ready, e_ln_step)
                rows_move(g, 2)

            edge_group(0)
            with pool.Fori(1, EG) as e:
                edge_group(e)
            with pool.Fori(GROUP_SCAN0, NG - 2) as g:
                rows_next(g + 1)
                indices(g)
                rows_move(g, 2)
            rows_next(NG - 1)
            pool.tensor_copy(idx_s[:, :], perm_s[:, T * (NG - 2):T * (NG - 1)]).then_inc(idx_ready, 1)
            pool.wait_ge(idx_ready, 2 * (NG - 2) + 1)
            rows_move(NG - 2, 1)
            pool.tensor_copy(idx_s[:, :], perm_s[:, T * (NG - 1):T * NG]).then_inc(idx_ready, 1)
            pool.wait_ge(idx_ready, 2 * (NG - 2) + 2)
            rows_move(NG - 1, 0)
            for t in range(T):
                pool.wait_ge(rows_out[t], 16 * NG)

        @block.tensor
        def _(pe):
            pe.wait_ge(const_done, CONSTS)
            pe.wait_ge(hot_ready, 1)
            for j in range(ET):
                mm = pe.matmul(pst[0][:, 0:NJ], hot_p[0:R, j, :], hot_j[0:R, j, :], start=(j == 0), stop=(j == ET - 1))
            mm.then_inc(count_done, 1)
            pe.wait_ge(rowtot_ready, 1)
            pe.matmul(pst[1][:, 0:1], before[:, :], tab[:, 1, NJ - 1:NJ], start=True, stop=True).then_inc(offset_done, 1)
            for b in range(NJ // BJ):
                pe.wait_ge(hot_ready, b + 2)
                for j in range(BJ):
                    mm = pe.matmul(pst[0][0:R, 128:128 + NJ], ring_b[:, b % 2, j, :], ring_a[:, b % 2, j, :],
                                   start=(b == 0 and j == 0), stop=(b == NJ // BJ - 1 and j == BJ - 1))
                mm.then_inc(hot_used, 1)
                if b >= 2:
                    c = b - 2
                    pe.wait_ge(abs_ready, c + 1)
                    for i, bank in enumerate((ps2[0][:, 0, :], ps2[0][:, 1, :], ps2[1][:, 0, :])):
                        mm = pe.matmul(bank, ones16[:, :], w1abs[:, c % 2, 512 * i:512 * (i + 1)],
                                       start=(c == 0), stop=(c == KC - 1))
                    mm.then_inc(abs_used, 1)
            pe.wait_ge(in_vecs, 80)
            for i in range(5):
                mm = pe.transpose(ps2[1][:, 1, MC * i:MC * (i + 1)], vecs[:, i, :], ident[0:MC, 0:MC])
            mm.then_inc(vecs_done, 1)
            pe.wait_ge(s1_ready, 1)
            for m in range(MC):
                mm = pe.matmul(ps2[1][:, 1, 64 + m:65 + m], s1row[0:1, P * m:P * (m + 1)], ones[0:1, 0:1], start=True, stop=True)
            mm.then_inc(s1col_done, 1)

            def transpose_chunk(q, c):
                if c == 0:
                    wait(pe, h_ready, T * (q + 1))
                wait(pe, xl_ready, KC * q + c - 1)
                for t in range(T):
                    mm = pe.transpose(pst[c % 2][:, R * t:R * (t + 1)], hrow[0:R, t, P * c:P * (c + 1)], ident[0:R, 0:R])
                mm.then_inc(tr_done, 1)

            def edge_chunk(e, q, c):
                if c == 0:
                    wait(pe, e_h_ready, T * (e + 1))
                    wait(pe, xl_ready, KC * (q + 1))
                if c >= 2:
                    wait(pe, e_msg_ready, KC * e + c - 1)
                for t in range(T):
                    mm = pe.transpose(pst[c % 2][:, R * t:R * (t + 1)], xedge[0:R, t, P * c:P * (c + 1)], ident[0:R, 0:R])
                mm.then_inc(e_tr_done, 1)

            def first_product(g):
                wait(pe, xl_ready, KC * (g + 1))
                for m in range(MC):
                    wait(pe, al_ready, MC * g + m - 1)
                    col = slice(P * m, P * (m + 1))
                    for k in range(KC):
                        pe.matmul(ps1[m % 2][:, 0:GW], w1h[:, k, col], xth[:, k, :], start=(k == 0), stop=False)
                        pe.matmul(ps1[m % 2][:, 0:GW], w1h[:, k, col], xtl[:, k, :], start=False, stop=False)
                        mm = pe.matmul(ps1[m % 2][:, 0:GW], w1l[:, k, col], xth[:, k, :], start=False, stop=(k == KC - 1))
                    mm.then_inc(mm1_done, 1)

            def second_product(g, t, half):
                o = ps2[t % 2]
                if half == 0:
                    wait(pe, fin_ready, T * g + t - 1)
                for m in range(MC // 2 * half, MC // 2 * (half + 1)):
                    if t == 0:
                        wait(pe, al_ready, MC * g + m + 1)
                    if isinstance(g, int) and g == 0 and t == 0:
                        pe.wait_ge(w2l_ready, m + 1)
                    rows_h, rows_l = ah[:, m, R * t:R * t + P], al[:, m, R * t:R * t + P]
                    lo, hi = slice(0, HALF), slice(HALF, D)
                    s, e = m == 0, m == MC - 1
                    pe.matmul(o[:, 0, 0:HALF], rows_h, w2h[:, m, lo], start=s, stop=False)
                    pe.matmul(o[:, 1, 0:HALF], rows_h, w2h[:, m, hi], start=s, stop=False)
                    pe.matmul(o[:, 0, 0:HALF], rows_h, w2l[:, m, lo], start=False, stop=False)
                    pe.matmul(o[:, 1, 0:HALF], rows_h, w2l[:, m, hi], start=False, stop=False)
                    pe.matmul(o[:, 0, 0:HALF], rows_l, w2h[:, m, lo], start=False, stop=e)
                    mm = pe.matmul(o[:, 1, 0:HALF], rows_l, w2h[:, m, hi], start=False, stop=e)
                if half == 1:
                    mm.then_inc(mm2_done, 1)

            def group(g, nxt=True, edges=None, sort=None):
                first_product(g)
                if edges is not None:
                    wait(pe, e_msg_ready, KC * edges)
                for slot in range(2 * T):
                    if nxt and slot < 3:
                        transpose_chunk(g + 1, 2 * slot)
                        transpose_chunk(g + 1, 2 * slot + 1)
                    if edges is not None and 4 <= slot < 7:
                        edge_chunk(edges, g + 1, 2 * (slot - 4))
                        edge_chunk(edges, g + 1, 2 * (slot - 4) + 1)
                    if sort and slot in sort:
                        sort[slot]()
                    second_product(g, slot // 2, slot % 2)

            def sort_edges():
                pe.wait_ge(sort_hot, 1)
                pe.wait_ge(xl_ready, KC * 3)
                for j in range(ET):
                    mm = pe.matmul(pst[0][0:R, 0:2 * ET], slot_hot[:, j, :], tile_hot[:, j, :, :].rearrange("p s a -> p (s a)"),
                                   start=(j == 0), stop=(j == ET - 1))
                mm.then_inc(sorted_done, 1)

            def dst_rows():
                pe.wait_ge(diag_ready, 1)
                for i in range(ET // T):
                    wait(pe, row_used, i - 1)
                    pe.matmul(pst[i % 2][:, 0:GW], ones[0:R, :], dst_diag[:, T * i:T * (i + 1), :].rearrange("p a b -> p (a b)"),
                              start=True, stop=True).then_inc(row_done, 1)

            def pick_free():
                pe.wait_ge(pick_hot, 1)
                for i in range(ET):
                    sl = slice(R * i, R * (i + 1))
                    pe.matmul(pst[0][0:R, ET * i:ET * (i + 1)], s2[0:R, sl], perm_f[0:R, FREE_T:NT], start=True, stop=True)
                    pe.matmul(pst[0][0:R, 400 + i:401 + i], s0[0:1, sl], ones[0:1, 0:1], start=True, stop=True)
                    mm = pe.matmul(pst[0][0:R, 420 + i:421 + i], first[0:1, 1 + R * i:1 + R * (i + 1)], ones16[0:1, 0:1],
                                   start=True, stop=True)
                mm.then_inc(picks_done, 1)

            for c in range(KC):
                transpose_chunk(0, c)
            pe.wait_ge(w1l_ready, KC)
            pe.wait_ge(pads_zero, 2)
            group(0)
            group(1, sort={4: sort_edges, 5: dst_rows, 7: pick_free})
            pe.wait_ge(picks_copied, 1)
            group(GROUP_EDGE0, edges=0)
            with pe.Fori(1, EG) as e:
                group(e + GROUP_EDGE0, edges=e)
            pe.wait_ge(e_msg_ready, KC * EG)
            with pe.Fori(GROUP_SCAN0, NG - 1) as g:
                group(g)
            group(NG - 1, nxt=False)

        @block.scalar
        def _(act):
            for c in range(KC):
                act.wait_ge(in_w1[c], 16)
                wait(act, abs_used, c - 1)
                act.activation(w1abs[:, c % 2, :], wst1[:, c, :], ACT.Abs).then_inc(abs_ready, 1)

            def w1_high(c):
                act.wait_ge(w1s_dve if c < 4 else w1s_pool, c + 1 if c < 4 else c - 3)
                act.activation(w1h[:, c, :], wst1[:, c, :], ACT.Copy).then_inc(w1h_ready, 1)

            def norm_rows(q, t):
                wait(act, ln_step, 4 * (T * q + t + 1))
                wait(act, tr_done, KC * q)
                wait(act, res_ready, T * (q - 1) + t + 1)
                act.activation(hrow[:, t, :], xin[:, t, :], ACT.Relu, scale=ln[:, t, 0:1], bias=ln[:, t, 1:2]).then_inc(h_ready, 1)

            def edge_norm_rows(e):
                for t in range(T):
                    wait(act, e_ln_step, 4 * (T * e + t + 1))
                    act.activation(xedge[:, t, :], xedge[:, t, :], ACT.Relu, scale=ln_e[:, t, 0:1],
                                   bias=ln_e[:, t, 1:2]).then_inc(e_h_ready, 1)

            def x_high(q, c, tail):
                wait(act, sum_done if tail else tr_done, KC * (q - TAIL) + c + 1 if tail else KC * q + c + 1)
                source = xsum[:, c % 2, :] if tail else pst[c % 2][:, 0:GW]
                act.activation(xth[:, c, :], source, ACT.Copy, scale=XS).then_inc(xh_ready, 1)

            def hidden(g, m):
                wait(act, mm1_done, MC * g + m + 1)
                act.activation(ps1[m % 2][:, 0:GW], ps1[m % 2][:, 0:GW], ACT.Relu, scale=vcol[:, 13, m:m + 1],
                               bias=vcol[:, 14, m:m + 1]).then_inc(act_done, 1)
                wait(act, act_done, MC * g + m + 1)
                act.activation(ah[:, m, 0:GW], ps1[m % 2][:, 0:GW], ACT.Copy).then_inc(ah_ready, 1)

            def w2_high(m):
                act.activation(w2h[:, m, :], wst2[:, m, :], ACT.Copy, scale=vcol[:, 15, m:m + 1]).then_inc(w2h_ready, 1)

            for c in range(KC):
                w1_high(c)
            for t in range(T):
                norm_rows(0, t)
            for c in range(KC):
                x_high(0, c, False)
            act.wait_ge(bn_ready, 1)

            def group(g, tail=False, nxt=True, edges=None, scan=None):
                for m in range(MC):
                    hidden(g, m)
                    if nxt and m in (3, 5, 7, 9):
                        norm_rows(g + 1, (m - 3) // 2)
                    if isinstance(g, int) and g == 0 and m == 8:
                        act.wait_ge(w2scale_ready, 1)
                    if isinstance(g, int) and g == 0 and m >= 8:
                        for i in range(3 * (m - 8), 3 * (m - 7)):
                            w2_high(i)
                if scan is not None:
                    wait(act, msg_in, 16 * (scan + 1))
                    act.activation(s1, s0, ACT.Copy, scale=tcol[:, 0:1]).then_inc(scan_act, 1)
                for c in range(KC if nxt else 0):
                    if edges is not None and c == 4:
                        edge_norm_rows(edges)
                    if scan is not None and c == 4:
                        wait(act, scan_step, SCAN_STEPS * scan + 3)
                        act.activation(s1, s1, ACT.Exp).then_inc(scan_act, 1)
                    x_high(g + 1, c, tail)

            group(0)
            act.wait_ge(in_t, 16)
            group(1)
            group(GROUP_EDGE0, edges=0)
            with act.Fori(1, EG) as e:
                group(e + GROUP_EDGE0, edges=e)
            group(GROUP_SCAN0, scan=0)
            with act.Fori(1, KC) as c:
                group(c + GROUP_SCAN0, scan=c)
            group(GROUP_PLAIN)
            with act.Fori(GROUP_PLAIN + 1, NG - 1) as g:
                group(g, tail=True)
            group(NG - 1, nxt=False)

        @block.vector
        def _(dve):
            step = [0]

            def link(ins):
                step[0] += 1
                ins.then_inc(dve_step, 1)
                dve.wait_ge(dve_step, step[0])

            def power_of_two(ap):
                bits = ap.bitcast(i32)
                link(dve.tensor_scalar(bits, bits, EXP_BITS, EXP_BITS, ALU.bitwise_and, ALU.bitwise_xor))
                link(dve.tensor_scalar(ap, ap, 8192.0, None, ALU.mult))

            def divmod_rows(q_i, q_f, r, value):
                link(dve.tensor_scalar(q_i, value, 62.0, 1.0 / R, ALU.subtract, ALU.mult))
                link(dve.tensor_copy(q_f, q_i))
                link(dve.scalar_tensor_tensor(r, q_f, -float(R), value, ALU.mult, ALU.add))

            dve.wait_ge(const_done, CONSTS)
            dve.wait_ge(in_edges, 32)
            e_in, e_out = edge_i[0:R, :, :], edge_f[0:R, :, :]
            link(dve.tensor_scalar(e_in[:, 2, :], e_in[:, 1, :], 7, None, ALU.logical_shift_right))
            link(dve.tensor_scalar(e_in[:, 3, :], e_in[:, 1, :], 127, None, ALU.bitwise_and))
            link(dve.tensor_copy(e_out, e_in))
            dve.tensor_tensor(hot_p[0:R, :, :], spread(lane[0:R, :], [R, ET, P], 1), spread(e_out[:, 3, :], [R, ET, P], 2), ALU.is_equal)
            dve.tensor_tensor(hot_j[0:R, :, :], spread(lane[0:R, 0:NJ], [R, ET, NJ], 1), spread(e_out[:, 2, :], [R, ET, NJ], 2),
                              ALU.is_equal).then_inc(hot_ready, 1)
            valid, rank_in, free, far, rank, q_f, rb = (tab[:, i, :] for i in range(7))
            link(dve.tensor_scalar(valid, node[:, :], float(N), None, ALU.is_lt))
            dve.wait_ge(count_done, 1)
            link(dve.scalar_tensor_tensor(free, pst[0][:, 0:NJ], 0.0, valid, ALU.is_equal, ALU.mult))
            dve.tensor_tensor_scan(rank_in, ones[:, 0:NJ], free, 0.0, ALU.mult, ALU.add).then_inc(rowtot_ready, 1)
            dve.wait_ge(rowtot_ready, 1)
            link(dve.tensor_scalar(far, free, -float(NOWHERE), float(NOWHERE) - 1.0, ALU.mult, ALU.add))
            dve.wait_ge(offset_done, 1)
            link(dve.tensor_copy(scol[:, 6:7], pst[1][:, 0:1]))
            link(dve.scalar_tensor_tensor(rank, rank_in, scol[:, 6:7], far, ALU.add, ALU.add))
            divmod_rows(tab_i[:, :], q_f, rb, rank)
            for b in range(NJ // BJ):
                wait(dve, hot_used, b - 1)
                for j in range(BJ):
                    n = BJ * b + j
                    dve.tensor_scalar(ring_b[:, b % 2, j, :], lane[:, 0:R], rb[:, n:n + 1], node[:, n:n + 1], ALU.is_equal, ALU.mult)
                dve.tensor_tensor(ring_a[:, b % 2, :, :], spread(lane[:, 0:NJ], [P, BJ, NJ], 1),
                                  spread(q_f[:, BJ * b:BJ * (b + 1)], [P, BJ, NJ], 2), ALU.is_equal).then_inc(hot_ready, 1)
            dve.wait_ge(hot_used, NJ // BJ)
            link(dve.tensor_copy(perm_f[0:R, :], pst[0][0:R, 128:128 + NJ]))
            dve.tensor_copy(perm_g[0:R, 0:FREE_T], perm_f[0:R, 0:FREE_T])
            dve.tensor_copy(perm_s[0:R, 0:FREE_T], perm_f[0:R, 0:FREE_T]).then_inc(perm_ready, 1)

            dve.wait_ge(abs_used, KC)
            for i, bank in enumerate((ps2[0][:, 0, :], ps2[0][:, 1, :], ps2[1][:, 0, :])):
                last = dve.tensor_scalar(s1row[:, 512 * i:512 * (i + 1)], bank, 1e-30, None, ALU.max)
            link(last)
            bits = s1row.bitcast(i32)
            link(dve.tensor_scalar(bits, bits, EXP_BITS, EXP_BITS, ALU.bitwise_and, ALU.bitwise_xor))
            dve.tensor_scalar(s1row, s1row, 8192.0, None, ALU.mult).then_inc(s1_ready, 1)
            dve.wait_ge(s1_ready, 1)
            for c in range(4):
                dve.tensor_tensor(wst1[:, c, :], wst1[:, c, :], s1row, ALU.mult).then_inc(w1s_dve, 1)

            def statistics(q, t, source, raw, m, s_in, s_raw, s_mv):
                wait(dve, s_in[t], 16 * (q + 1))
                dve.bn_stats(raw[:, t, 0:6], source[:, t, 0:HALF])
                dve.bn_stats(raw[:, t, 6:12], source[:, t, HALF:D]).then_inc(s_raw, 1)
                wait_turn(dve, s_raw, T * q + t + 1, dve_turn)
                dve.bn_aggr(m[:, t, :], raw[:, t, :]).then_inc(s_mv, 1)

            for t in range(T):
                statistics(0, t, xin, bnraw, mv, rows_in, bn_raw, mv_ready)

            dve.wait_ge(vecs_done, 1)
            dve.wait_ge(s1col_done, 1)
            link(dve.tensor_copy(vcol[:, 0:5, :], ps2[1][:, 1, 0:5 * MC].rearrange("p (i m) -> p i m", i=5)))
            vb1, vgamma, vbeta, vmean, vvar, v_eps, v_rsqrt, v_inv, v_bias, v_s1, v_unscale, v_bound, v_ca, v_scale, v_shift, v_w2 = \
                (vcol[:, i, :] for i in range(16))
            dve.tensor_scalar(v_eps, vvar, EPS_BN, None, ALU.add).then_inc(varp_ready, 1)
            link(dve.tensor_tensor(v_bias, vb1, vmean, ALU.subtract))
            link(dve.tensor_copy(v_s1, ps2[1][:, 1, 64:64 + MC]))
            link(dve.reciprocal(v_unscale, v_s1))
            dve.wait_ge(pow_ready, 1)
            link(dve.tensor_tensor(v_inv, v_rsqrt, vgamma, ALU.mult))
            link(dve.tensor_tensor(v_bias, v_bias, v_inv, ALU.mult))
            link(dve.tensor_tensor(v_bias, v_bias, vbeta, ALU.add))
            link(dve.scalar_tensor_tensor(v_bound, v_inv, -1.0, v_inv, ALU.mult, ALU.max))
            link(dve.scalar_tensor_tensor(v_bound, v_bound, 1.02 * XMAX * 2.0 ** 15, v_unscale, ALU.mult, ALU.mult))
            link(dve.scalar_tensor_tensor(v_ca, v_bias, -1.0, v_bias, ALU.mult, ALU.max))
            link(dve.tensor_scalar(v_bound, v_bound, 1e-30, None, ALU.max))
            link(dve.tensor_tensor(v_ca, v_ca, v_bound, ALU.add))
            power_of_two(v_ca)
            link(dve.tensor_tensor(v_scale, v_inv, v_ca, ALU.mult))
            link(dve.scalar_tensor_tensor(v_scale, v_scale, 1.0 / XS, v_unscale, ALU.mult, ALU.mult))
            link(dve.tensor_tensor(v_shift, v_bias, v_ca, ALU.mult))
            dve.reciprocal(v_bound, v_ca).then_inc(bn_ready, 1)

            for c in range(KC):
                dve.wait_ge(w1h_ready, c + 1)
                dve.tensor_tensor(w1l[:, c, :], wst1[:, c, :], w1h[:, c, :], ALU.subtract).then_inc(w1l_ready, 1)

            def x_sum(q, c):
                wait(dve, tr_done, KC * q + c + 1)
                wait(dve, agg_back, 16 * (q - TAIL + 1))
                dve.tensor_tensor(xsum[:, c % 2, :], pst[c % 2][:, 0:GW], agg_in[:, c, :], ALU.add).then_inc(sum_done, 1)

            def x_low(q, c, tail=False):
                wait(dve, xh_ready, KC * q + c + 1)
                source = xsum[:, c % 2, :] if tail else pst[c % 2][:, 0:GW]
                dve.scalar_tensor_tensor(xtl[:, c, :], source, XS, xth[:, c, :], ALU.mult, ALU.subtract).then_inc(xl_ready, 1)

            def hidden_low(g, m):
                wait(dve, ah_ready, MC * g + m + 1)
                dve.tensor_tensor(al[:, m, 0:GW], ps1[m % 2][:, 0:GW], ah[:, m, 0:GW], ALU.subtract).then_inc(al_ready, 1)

            def finish(g, t):
                wait(dve, base_ready, T * g + t + 1)
                wait(dve, mm2_done, T * g + t + 1)
                rows2 = base[:, t, :].rearrange("p (h n) -> p h n", h=2)
                dve.scalar_tensor_tensor(rows2, ps2[t % 2][:, :, 0:HALF], scol[:, 3:4], rows2, ALU.mult, ALU.add).then_inc(fin_ready, 1)

            def w2_max(q):
                dve.wait_ge(in_w2[q], 16)
                link(dve.tensor_reduce(pcol[:, 0, 4 * q:4 * q + 4], wst2[:, 4 * q:4 * q + 4, :], AX.X, ALU.max, apply_absolute_value=True))

            def w2_max_rows():
                link(dve.tensor_tensor(pcol[:, 1, :], pcol[:, 0, :], v_bound, ALU.mult))
                dve.tensor_reduce(scol[:, 0:1], pcol[:, 1, :], AX.X, ALU.max).then_inc(w2max_ready, 1)

            def w2_scale():
                dve.wait_ge(w2max_all, 1)
                link(dve.tensor_scalar(scol[:, 2:3], scol[:, 1:2], 1e-30, None, ALU.max))
                power_of_two(scol[:, 2:3])
                link(dve.reciprocal(scol[:, 3:4], scol[:, 2:3]))
                dve.tensor_scalar(v_w2, v_bound, scol[:, 2:3], None, ALU.mult).then_inc(w2scale_ready, 1)
                dve.wait_ge(w2scale_ready, 1)

            def w2_low(m):
                dve.wait_ge(w2h_ready, m + 1)
                dve.scalar_tensor_tensor(w2l[:, m, :], wst2[:, m, :], v_w2[:, m:m + 1], w2h[:, m, :],
                                         ALU.mult, ALU.subtract).then_inc(w2l_ready, 1)

            sor_src, sor_dst = sorted_e[0:R, 0, :], sorted_e[0:R, 1, :]

            def count_setup():
                dve.wait_ge(in_dstrow, 16)
                dve.memset(count3[:, :, :], 0.0)
                link(dve.tensor_copy(dst_cols, s0[0:R, :].bitcast(i32).rearrange("p (q j) -> p j q", j=ET)))
                link(dve.tensor_tensor(dst_tied, dst_cols, spread(tie[0:R, 0:R], [R, ET, R], 1), ALU.add))

            def count(j):
                mine = edge_f[0:R, 1, j:j + 1]
                junk = s0[0:R, :].rearrange("p (j q) -> p j q", j=ET)
                if j > 0:
                    link(dve.tensor_scalar(junk[:, 0:j, :], dst_cols[:, 0:j, :], mine, 0.0, ALU.is_le, ALU.add,
                                      accum_out=count3[0:R, 0, j:j + 1]))
                if j < ET - 1:
                    link(dve.tensor_scalar(junk[:, j + 1:ET, :], dst_cols[:, j + 1:ET, :], mine, 0.0, ALU.is_lt, ALU.add,
                                      accum_out=count3[0:R, 1, j:j + 1]))
                link(dve.tensor_scalar(junk[:, j, :], dst_tied[:, j, :], mine, 0.0, ALU.is_lt, ALU.add,
                                  accum_out=count3[0:R, 2, j:j + 1]))

            def place_edges():
                a, b, c = (count3[0:R, i, :] for i in range(3))
                link(dve.tensor_tensor(a, a, b, ALU.add))
                link(dve.tensor_tensor(a, a, c, ALU.add))
                divmod_rows(edge_i[0:R, 2, :], b, c, a)
                link(dve.tensor_tensor(slot_hot, spread(lane[0:R, 0:R], [R, ET, R], 1), spread(c, [R, ET, R], 2), ALU.is_equal))
                link(dve.tensor_tensor(tile_eq, spread(lane[0:R, 0:ET], [R, ET, ET], 1), spread(b, [R, ET, ET], 2), ALU.is_equal))
                for i in range(2):
                    last = dve.tensor_tensor(tile_hot[:, :, i, :], tile_eq, spread(edge_f[0:R, i, :], [R, ET, ET], 2), ALU.mult)
                last.then_inc(sort_hot, 1)

            def mark_segments():
                dve.wait_ge(sorted_done, 1)
                link(dve.tensor_copy(sorted_e[0:R, :, :], pst[0][0:R, 0:2 * ET].rearrange("p (s a) -> p s a", s=2)))
                link(dve.tensor_copy(src_g[0:R, :], sor_src))
                dve.tensor_tensor(dst_diag, spread(ident[0:R, 0:R], [R, ET, R], 1), spread(sor_dst, [R, ET, R], 2),
                                  ALU.mult).then_inc(diag_ready, 1)
                for i in range(ET // T):
                    dve.wait_ge(row_done, i + 1)
                    dve.tensor_copy(s0[:, GW * i:GW * (i + 1)], pst[i % 2][:, 0:GW]).then_inc(row_used, 1)
                dve.wait_ge(row_used, ET // T)
                dve.memset(first[:, 0:1], 1.0)
                dve.memset(first[:, E:E + 1], 1.0)
                link(dve.tensor_tensor(first[:, 1:E], s0[:, 1:E], s0[:, 0:E - 1], ALU.not_equal))
                link(dve.tensor_scalar(keep[:, 0:E + 1], first[:, 0:E + 1], -1.0, 1.0, ALU.mult, ALU.add))
                link(dve.tensor_scalar(cut[:, 0:E + 1], first[:, 0:E + 1], -3e38, None, ALU.mult))
                link(dve.tensor_tensor_scan(s1, keep[:, 1:E + 1], keep[:, 1:E + 1], 0.0, ALU.add, ALU.max))
                q_int = s2.bitcast(i32)
                link(dve.tensor_scalar(q_int, s1, 63.0, 1.0 / R, ALU.subtract, ALU.mult))
                link(dve.tensor_copy(s0, q_int))
                link(dve.scalar_tensor_tensor(s1, s0, -float(R), s1, ALU.mult, ALU.add))
                dve.tensor_scalar(s2, s1, part1[:, 0:1], None, ALU.is_equal).then_inc(pick_hot, 1)

            def place_tail():
                dve.wait_ge(picks_done, 1)
                dve.tensor_copy(picks, pst[0][0:R, 0:440]).then_inc(picks_copied, 1)
                dve.wait_ge(picks_copied, 1)
                cube = lambda i: s1[0:R, 500 * i:500 * i + ET * ET].rearrange("p (i a) -> p i a", i=ET)
                col = lambda i: s1[0:R, 1500 + ET * i:1500 + ET * (i + 1)]
                link(dve.tensor_tensor(cube(1), spread(lane[0:R, 0:ET], [R, ET, ET], 1), spread(picks[:, 400:420], [R, ET, ET], 2),
                                       ALU.is_equal))
                link(dve.tensor_tensor(cube(2), cube(1), picks[:, 0:400].rearrange("p (i a) -> p i a", i=ET), ALU.mult))
                link(dve.tensor_reduce(col(0), cube(2), AX.X, ALU.add))
                link(dve.tensor_tensor(col(1), sor_dst, col(0), ALU.subtract))
                link(dve.tensor_tensor(col(1), col(1), picks[:, 420:440], ALU.mult))
                link(dve.tensor_tensor(col(2), col(1), col(0), ALU.add))
                dve.tensor_copy(perm_g[0:R, FREE_T:NT], col(2))
                dve.tensor_copy(perm_s[0:R, FREE_T:NT], col(2)).then_inc(perm_ready, 1)

            def edge_message(e, c):
                wait(dve, e_tr_done, KC * e + c + 1)
                wait(dve, e_msg_out[c % 2], 16 * (KC // 2 * e + c // 2))
                dve.tensor_scalar(emsg[:, c % 2, :], pst[c % 2][:, 0:GW], EPS_MSG, None, ALU.add).then_inc(e_msg_ready, 1)

            def scan(c, at, ins):
                ins.then_inc(scan_step, 1)
                wait(dve, scan_step, SCAN_STEPS * c + at)

            def scan_max(c):
                wait(dve, scan_act, 2 * c + 1)
                scan(c, 1, dve.tensor_tensor_scan(s2, cut[:, 0:E], s1, 0.0, ALU.add, ALU.max))
                scan(c, 2, dve.tensor_tensor_scan(s2[:, ::-1], cut[:, 1:E + 1][:, ::-1], s2[:, ::-1], 0.0, ALU.add, ALU.max))

            def scan_shift(c):
                scan(c, 3, dve.tensor_tensor(s1, s1, s2, ALU.subtract))

            def scan_sums(c):
                wait(dve, scan_act, 2 * c + 2)
                scan(c, 4, dve.tensor_tensor(s0, s0, s1, ALU.mult))
                scan(c, 5, dve.tensor_tensor_scan(s2, keep[:, 0:E], s1, 0.0, ALU.mult, ALU.add))
                scan(c, 6, dve.tensor_tensor_scan(s1, keep[:, 0:E], s0, 0.0, ALU.mult, ALU.add))
                scan(c, 7, dve.tensor_scalar(s2, s2, EPS_SUM, None, ALU.add))

            def scan_reciprocal(c, parts):
                for i in parts:
                    ins = dve.reciprocal(s2[:, GW * i:GW * (i + 1)], s2[:, GW * i:GW * (i + 1)])
                return ins

            def scan_quotient(c, ins):
                scan(c, 8, ins)
                scan(c, 9, dve.tensor_tensor(s1, s1, s2, ALU.mult))
                scan(c, 10, dve.tensor_tensor(s1, s1, first[:, 1:E + 1], ALU.mult))

            def group(g, tail=False, nxt=True, edges=None, scans=None, sort=None):
                for m in range(MC):
                    hidden_low(g, m)
                    if nxt and m in (2, 4, 6, 8):
                        statistics(g + 1, (m - 2) // 2, xin, bnraw, mv, rows_in, bn_raw, mv_ready)
                    if sort == 0:
                        if 5 <= m < 8:
                            w2_max(m - 5)
                        if m == 7:
                            w2_max_rows()
                        if m == 8:
                            w2_scale()
                        if m >= 9:
                            for i in range(3 * (m - 9), 3 * (m - 8)):
                                w2_low(i)
                if sort == 0:
                    for i in range(9, MC):
                        w2_low(i)

                def low(*chunks):
                    for c in chunks if nxt else ():
                        if tail and c == 0:
                            x_sum(g + 1, 0)
                            x_sum(g + 1, 1)
                        x_low(g + 1, c, tail)
                        if tail and c + 2 < KC:
                            x_sum(g + 1, c + 2)

                def counts(lo, hi):
                    for j in range(lo, hi):
                        count(j)

                low(0, 1)
                if edges is not None:
                    for t in range(T):
                        statistics(edges, t, xedge, bnraw_e, mv_e, e_rows_in, e_bn_raw, e_mv_ready)
                if scans is not None:
                    scan_max(scans)
                if sort == 1:
                    counts(14, 17)
                low(2, 3)
                if scans is not None:
                    scan_shift(scans)
                if sort == 0:
                    count_setup()
                    counts(0, 2)
                finish(g, 0)
                low(4, 5)
                if scans is not None:
                    scan_sums(scans)
                if sort == 0:
                    counts(2, 6)
                if sort == 1:
                    counts(17, ET)
                    place_edges()
                finish(g, 1)
                if edges is not None:
                    for c in range(4):
                        edge_message(edges, c)
                if scans is not None:
                    scan_reciprocal(scans, range(0, 3))
                if sort == 0:
                    counts(6, 10)
                if sort == 1:
                    mark_segments()
                finish(g, 2)
                if edges is not None:
                    for c in range(4, KC):
                        edge_message(edges, c)
                if scans is not None:
                    scan_quotient(scans, scan_reciprocal(scans, range(3, 5)))
                if sort == 0:
                    counts(10, 14)
                if sort == 1:
                    place_tail()
                finish(g, 3)

            for c in range(KC):
                x_low(0, c)
            group(0, sort=0)
            group(1, sort=1)
            group(GROUP_EDGE0, edges=0)
            with dve.Fori(1, EG) as e:
                group(e + GROUP_EDGE0, edges=e)
            group(GROUP_SCAN0, scans=0)
            with dve.Fori(1, KC) as c:
                group(c + GROUP_SCAN0, scans=c)
            group(GROUP_PLAIN)
            with dve.Fori(GROUP_PLAIN + 1, NG - 1) as g:
                group(g, tail=True)
            group(NG - 1, nxt=False)


_INS = ["x", "src", "dst", "L0_gnn_t", "L0_gnn_W1", "L0_gnn_b1", "L0_gnn_bn_gamma", "L0_gnn_bn_beta", "L0_gnn_bn_mean",
        "L0_gnn_bn_var", "L0_gnn_W2", "L0_gnn_b2"]


def kernel(**inputs):
    import numpy as np
    import concourse.bacc as bacc
    from concourse.bass_utils import run_bass_kernel_spmd

    nc = bacc.Bacc("TRN2", target_bir_lowering=False, num_devices=1)
    arrays, args = {}, []
    for name in _INS:
        a = np.ascontiguousarray(inputs[name])
        if a.ndim == 0:
            a = a.reshape(1)
        arrays[name + "_dram"] = a
        args.append(nc.dram_tensor(name + "_dram", a.shape, mybir.dt.from_np(a.dtype), kind="ExternalInput").ap())
    out = nc.dram_tensor("out_dram", inputs["x"].shape, mybir.dt.float32, kind="ExternalOutput").ap()
    gnn_layer(nc, *args, out)
    r = run_bass_kernel_spmd(nc, [arrays], core_ids=[0])
    return r.results[0]["out_dram"]
```

```python
from contextlib import ExitStack

import concourse.bass as bass
from concourse import mybir


def gnn_layer(nc, x, src, dst, t_in, W1, b1, gamma, beta, mean, var, W2, b2, out):
    f32, f16, bf16, i32 = mybir.dt.float32, mybir.dt.float16, mybir.dt.bfloat16, mybir.dt.int32
    ALU = mybir.AluOpType
    ACT = mybir.ActivationFunctionType
    AX = mybir.AxisListType
    LARGEST = bass.bass_isa.ReduceOp.max

    P = 128
    N, D = x.shape
    E = src.shape[0]
    HID = W1.shape[1]
    KC, MC = D // P, HID // P
    R, T = 125, 4
    GW = R * T
    NG = N // GW
    NT = NG * T
    ET = E // R
    FREE_T = NT - ET
    EG = ET // T
    TAIL = FREE_T // T
    NJ = 80
    HALF = D // 2
    EPS_MSG, EPS_BN, EPS_LN, EPS_SUM = 1e-7, 1e-5, 1e-5, 1e-16
    XS = 512.0
    XMAX = 55.5
    NOWHERE = 20000
    EXP_BITS = 0x7F800000
    CONSTS = 17
    SCAN_STEPS = 10
    W1C = 3
    W1W = HID // W1C
    GROUP_EDGE0 = 3
    GROUP_SCAN0 = GROUP_EDGE0 + EG
    assert NG * GW == N and ET * R == E and GROUP_SCAN0 + KC == TAIL - 1 and N < P * NJ and W1W == 512

    agg_dram = nc.dram_tensor("agg_scratch", (KC, P, E), f32, kind="Internal").ap()

    ctx = ExitStack()
    with ctx:
        def sb(name, shape, dt):
            return ctx.enter_context(nc.sbuf_tensor(name, shape, dt))

        def sem(name):
            return ctx.enter_context(nc.semaphore(name))

        w1h, w1l = sb("w1h", [P, KC, HID], f16), sb("w1l", [P, KC, HID], f16)
        w2h, w2l = sb("w2h", [P, MC, D], f16), sb("w2l", [P, MC, D], f16)
        xin = sb("xin", [P, T, D], f32)
        base = sb("base", [P, T, D], f32)
        hrow = sb("hrow", [P, T, D], f32)
        xth, xtl = sb("xth", [P, KC, GW], f16), sb("xtl", [P, KC, GW], f16)
        ah, al = sb("ah", [P, MC, 512], f16), sb("al", [P, MC, 512], f16)
        b2row = sb("b2row", [P, D], f32)
        xsum = sb("xsum", [P, 2, GW], f32)
        arena = sb("arena", [P, 11256], f32)
        s0, s1, s2 = (arena[:, E * i:E * (i + 1)] for i in range(3))
        mark = [arena[:, 7500 + 1252 * i:7500 + 1252 * (i + 1)].bitcast(bf16) for i in range(3)]
        first, keep, cut = mark

        ident = sb("ident", [P, P], f32)
        ones = sb("ones", [P, P], f32)
        ones16 = sb("ones16", [P, P], bf16)
        before = sb("before", [P, P], f32)
        tie = sb("tie", [P, P], f32)
        lane = sb("lane", [P, P], f32)
        node = sb("node", [P, NJ], f32)
        part0 = sb("part0", [P, 1], f32)
        part1 = sb("part1", [P, 1], f32)
        column16 = sb("column16", [P, NJ], bf16)
        edge16 = sb("edge16", [P, 2, ET], bf16)
        rank16 = sb("rank16", [P, 2, NJ], bf16)
        perm_f = sb("perm_f", [P, NJ], f32)
        perm2 = sb("perm2", [P, 2, NJ], f32)
        perm_g = sb("perm_g", [P, NT], i32)
        perm_s = sb("perm_s", [P, NT], i32)
        src_g = sb("src_g", [P, ET], i32)
        idx_g, idx_s, idx_e = sb("idx_g", [P, T], i32), sb("idx_s", [P, T], i32), sb("idx_e", [P, T], i32)
        edge_i = sb("edge_i", [P, 4, ET], i32)
        edge_f = sb("edge_f", [P, 4, ET], f32)
        tab = sb("tab", [P, 7, NJ], f32)
        tab_i = sb("tab_i", [P, NJ], i32)
        count3 = sb("count3", [P, 3, ET], f32)
        sorted_e = sb("sorted_e", [P, 2, ET], f32)
        vecs = sb("vecs", [MC, 5, P], f32)
        vcol = sb("vcol", [P, 16, MC], f32)
        pcol = sb("pcol", [P, 2, MC], f32)
        scol = sb("scol", [P, 8], f32)
        tcol = sb("tcol", [P, 1], f32)
        bnraw, bnraw_e = sb("bnraw", [P, T, 12], f32), sb("bnraw_e", [P, T, 12], f32)
        mv, mv_e = sb("mv", [P, T, 2], f32), sb("mv_e", [P, T, 2], f32)
        ln, ln_e = sb("ln", [P, T, 3], f32), sb("ln_e", [P, T, 3], f32)
        neghalf = sb("neghalf", [P, MC], f32)

        wst1 = arena[:, 0:KC * HID].rearrange("p (c n) -> p c n", c=KC)
        wst2 = arena[:, 0:MC * D].rearrange("p (m n) -> p m n", m=MC)
        base_flat = base[:, :, :].rearrange("p t n -> p (t n)")
        w1abs = base_flat[:, 0:HID].bitcast(bf16).rearrange("p (s n) -> p s n", s=2)
        s1row = base_flat[:, HID:2 * HID]
        ah_flat = ah[:, :, :].rearrange("p m n -> p (m n)")
        al_flat = al[:, :, :].rearrange("p m n -> p (m n)")
        lane16 = arena[:, KC * HID:KC * HID + P * ET // 2].bitcast(bf16).rearrange("p (b j) -> p b j", j=ET)
        hot_p = ah_flat[0:R, 0:ET * P].bitcast(bf16).rearrange("p (b j) -> p b j", j=ET)
        hot_j = ah_flat[0:R, ET * P:ET * (P + NJ)].bitcast(bf16).rearrange("p (b j) -> p b j", j=ET)
        BJ = 10
        ring_b = ah_flat[:, 0:2 * BJ * R].bitcast(bf16).rearrange("p (s b j) -> p s b j", s=2, j=BJ)
        ring_a = al_flat[:, 0:4 * BJ * NJ].bitcast(bf16).rearrange("p (s k b j) -> p s k b j", s=2, k=2, j=BJ)
        tile_of = al_flat[:, 4 * BJ * NJ:5 * BJ * NJ].bitcast(bf16).rearrange("p (b j) -> p b j", j=BJ)
        dst_cols = s1[0:R, :].rearrange("p (j q) -> p j q", j=ET)
        dst_tied = s2[0:R, :].rearrange("p (j q) -> p j q", j=ET)
        slot_hot = s2[0:R, :].rearrange("p (j b) -> p j b", j=ET)
        tile_hot = s0[0:R, 0:2 * ET * ET].rearrange("p (j s a) -> p j s a", j=ET, s=2)
        tile_eq = s0[0:R, 1000:1000 + ET * ET].rearrange("p (j a) -> p j a", j=ET)
        dst_diag = s1[0:R, :].rearrange("p (a b) -> p a b", a=ET)
        picks = s1[0:R, 0:440]
        xedge = arena[:, 0:T * D].rearrange("p (t n) -> p t n", t=T)
        emsg = arena[:, T * D:T * D + 2 * GW].rearrange("p (s n) -> p s n", s=2)
        agg_in = arena[:, 0:KC * GW].rearrange("p (c n) -> p c n", c=KC)

        def pb(name, shape, dt):
            return ctx.enter_context(nc.psum_tensor(name, shape, dt))

        ps1 = [pb(f"ps1_{i}", [P, 512], f32) for i in range(2)]
        pst = [pb(f"pst_{i}", [P, 512], f32) for i in range(2)]
        ps2 = [pb(f"ps2_{i}", [P, 2, 512], f32) for i in range(2)]

        in_edges, in_dstrow, in_vecs, in_b2, in_t = map(sem, ("in_edges", "in_dstrow", "in_vecs", "in_b2", "in_t"))
        in_w1 = [sem(f"in_w1_{c}") for c in range(KC)]
        in_w2 = [sem(f"in_w2_{q}") for q in range(3)]
        const_done = sem("const_done")
        dve_step = sem("dve_step")
        pool_turn = sem("pool_turn")
        dve_turn = sem("dve_turn")
        hot_ready, hot_used = sem("hot_ready"), sem("hot_used")
        count_done, offset_done = sem("count_done"), sem("offset_done")
        rowtot_ready = sem("rowtot_ready")
        perm_ready, pads_zero = sem("perm_ready"), sem("pads_zero")
        abs_ready, abs_used = sem("abs_ready"), sem("abs_used")
        s1_ready, w1s_dve, w1s_pool = sem("s1_ready"), sem("w1s_dve"), sem("w1s_pool")
        w1h_ready, w1l_ready = sem("w1h_ready"), sem("w1l_ready")
        vecs_done, s1col_done = sem("vecs_done"), sem("s1col_done")
        varp_ready, pow_ready, bn_ready = sem("varp_ready"), sem("pow_ready"), sem("bn_ready")
        w2max_ready, w2max_all, w2scale_ready = sem("w2max_ready"), sem("w2max_all"), sem("w2scale_ready")
        w2h_ready, w2l_ready = sem("w2h_ready"), sem("w2l_ready")
        sort_hot, sorted_done = sem("sort_hot"), sem("sorted_done")
        diag_ready, row_done, row_used = sem("diag_ready"), sem("row_done"), sem("row_used")
        pick_hot, picks_done = sem("pick_hot"), sem("picks_done")
        picks_copied = sem("picks_copied")
        rows_in = [sem(f"rows_in_{t}") for t in range(T)]
        rows_out = [sem(f"rows_out_{t}") for t in range(T)]
        idx_ready, bn_raw, mv_ready, ln_step = sem("idx_ready"), sem("bn_raw"), sem("mv_ready"), sem("ln_step")
        h_ready, res_ready, base_ready = sem("h_ready"), sem("res_ready"), sem("base_ready")
        tr_done, sum_done, xh_ready, xl_ready = sem("tr_done"), sem("sum_done"), sem("xh_ready"), sem("xl_ready")
        mm1_done, act_done, ah_ready, al_ready = sem("mm1_done"), sem("act_done"), sem("ah_ready"), sem("al_ready")
        mm2_done, fin_ready = sem("mm2_done"), sem("fin_ready")
        e_idx_ready = sem("e_idx_ready")
        e_rows_in = [sem(f"e_rows_in_{t}") for t in range(T)]
        e_bn_raw, e_mv_ready, e_ln_step, e_h_ready = map(sem, ("e_bn_raw", "e_mv_ready", "e_ln_step", "e_h_ready"))
        e_tr_done, e_msg_ready = sem("e_tr_done"), sem("e_msg_ready")
        e_msg_out = [sem(f"e_msg_out_{i}") for i in range(2)]
        msg_in, scan_step, scan_act, agg_out, agg_back = map(sem, ("msg_in", "scan_step", "scan_act", "agg_out", "agg_back"))

        def wait(eng, s, v):
            if not (isinstance(v, int) and v <= 0):
                eng.wait_ge(s, v)

        def wait_turn(eng, s, v, turn):
            if isinstance(v, int):
                wait(eng, s, v)
            else:
                eng.wait_ge(s, v)
                eng.sem_inc(turn, 1)

        def spread(ap, shape, axis):
            return ap.unsqueeze(axis).to_broadcast(shape)

        block = ctx.enter_context(nc.Block())

        @block.sync
        def _(sp):
            sp.dma_start(edge_i[0:R, 1, :], dst.rearrange("(p j) -> p j", j=ET)).then_inc(in_edges, 16)
            sp.dma_start(edge_i[0:R, 0, :], src.rearrange("(p j) -> p j", j=ET)).then_inc(in_edges, 16)
            for i, v in enumerate((b1, gamma, beta, mean, var)):
                sp.dma_start(vecs[:, i, :], v.rearrange("(m p) -> m p", p=P)).then_inc(in_vecs, 16)
            for c in range(KC):
                sp.dma_start(wst1[:, c, :], W1[P * c:P * (c + 1), :]).then_inc(in_w1[c], 16)
            sp.dma_start(b2row[:, :], b2.partition_broadcast(P)).then_inc(in_b2, 16)
            sp.dma_start(tcol[:, :], t_in.partition_broadcast(P)).then_inc(in_t, 16)
            sp.wait_ge(w1l_ready, W1C)
            for q in range(3):
                sp.dma_start(wst2[:, 4 * q:4 * q + 4, :],
                             W2[512 * q:512 * (q + 1), :].rearrange("(m p) n -> p m n", p=P)).then_inc(in_w2[q], 16)
            sp.wait_ge(w2l_ready, MC)
            sp.dma_start(s0[0:R, :].bitcast(i32), dst.partition_broadcast(R)).then_inc(in_dstrow, 16)

            def edge_group_out(e):
                for c in range(KC):
                    wait(sp, e_msg_ready, KC * e + c + 1)
                    sp.dma_start(agg_dram[c, :, bass.ds(GW * e, GW)], emsg[:, c % 2, :]).then_inc(e_msg_out[c % 2], 16)

            edge_group_out(0)
            with sp.Fori(1, EG) as e:
                edge_group_out(e)
            for i in range(2):
                sp.wait_ge(e_msg_out[i], 16 * EG * KC // 2)

            def scan_io(c):
                wait(sp, agg_out, 16 * c)
                sp.dma_start(s0, agg_dram[bass.ds(c, 1), :, :].rearrange("o p e -> (o p) e")).then_inc(msg_in, 16)
                wait(sp, scan_step, SCAN_STEPS * (c + 1))
                sp.dma_start(agg_dram[bass.ds(c, 1), :, :].rearrange("o p e -> (o p) e"), s1).then_inc(agg_out, 16)

            scan_io(0)
            with sp.Fori(1, KC) as c:
                scan_io(c)
            sp.wait_ge(agg_out, 16 * KC)

            def tail_group_in(e):
                wait(sp, sum_done, KC * e)
                sp.dma_start(agg_in, agg_dram[:, :, bass.ds(GW * e, GW)].rearrange("c p e -> p c e")).then_inc(agg_back, 16)

            tail_group_in(0)
            with sp.Fori(1, EG) as e:
                tail_group_in(e)

        @block.gpsimd
        def _(pool):
            bound = pool.to_reg(N - 1)

            def const(ins, steps=[0]):
                steps[0] += 1
                ins.then_inc(const_done, 1)
                return steps[0]

            const(pool.iota(lane16, pattern=[[1, P], [0, ET]], base=0, channel_multiplier=0, allow_small_or_imprecise_dtypes=True))
            const(pool.iota(column16[:, :], pattern=[[1, NJ]], base=0, channel_multiplier=0, allow_small_or_imprecise_dtypes=True))
            const(pool.iota(part0[:, :], pattern=[[1, 1]], base=0, channel_multiplier=1, allow_small_or_imprecise_dtypes=True))
            const(pool.iota(lane[:, :], pattern=[[1, P]], base=0, channel_multiplier=0, allow_small_or_imprecise_dtypes=True))
            const(pool.iota(node[:, :], pattern=[[P, NJ]], base=0, channel_multiplier=1, allow_small_or_imprecise_dtypes=True))
            const(pool.memset(ones[:, :], 1.0))
            const(pool.iota(part1[:, :], pattern=[[1, 1]], base=1, channel_multiplier=1, allow_small_or_imprecise_dtypes=True))
            const(pool.memset(tie[:, :], -0.5))
            const(pool.memset(ident[:, :], 0.0))
            const(pool.memset(neghalf[:, :], -0.5))
            n = const(pool.memset(ones16[:, :], 1.0))
            pool.wait_ge(const_done, n)
            const(pool.affine_select(out=before[:, :], in_=ones[:, :], compare_op=ALU.is_gt, fill=0.0,
                                     base=0, pattern=[[1, P]], channel_multiplier=-1))
            const(pool.affine_select(out=tie[:, :], in_=tie[:, :], compare_op=ALU.is_gt, fill=0.0,
                                     base=0, pattern=[[-1, P]], channel_multiplier=1))
            const(pool.affine_select(out=ident[:, :], in_=ident[:, :], compare_op=ALU.not_equal, fill=1.0,
                                     base=0, pattern=[[-1, P]], channel_multiplier=1))
            const(pool.memset(perm_g[:, :], 0))
            const(pool.memset(src_g[:, :], 0))
            n = const(pool.memset(perm_s[:, :], NOWHERE))
            assert n == CONSTS

            def gather(q, t, index):
                pool.indirect_dma_start(xin[:, t, :], None, x, bass.IndirectOffsetOnAxis(ap=index, axis=0),
                                        bounds_check=bound, oob_is_err=False).then_inc(rows_in[t], 16)

            def norm_tile(q, t, m, l, s_mv, s_step):
                at = 4 * (T * q + t)
                wait_turn(pool, s_mv, T * q + t + 1, pool_turn)
                pool.tensor_scalar(l[:, t, 2:3], m[:, t, 1:2], EPS_LN, None, ALU.add).then_inc(s_step, 1)
                wait_turn(pool, s_step, at + 1, pool_turn)
                pool.tensor_tensor(l[:, t, 0:1], l[:, t, 2:3], neghalf[:, 0:1], ALU.pow).then_inc(s_step, 1)
                wait_turn(pool, s_step, at + 2, pool_turn)
                pool.tensor_tensor(l[:, t, 2:3], m[:, t, 0:1], l[:, t, 0:1], ALU.mult).then_inc(s_step, 1)
                wait_turn(pool, s_step, at + 3, pool_turn)
                pool.tensor_scalar(l[:, t, 1:2], l[:, t, 2:3], -1.0, None, ALU.mult).then_inc(s_step, 1)

            def residual(q, t):
                wait_turn(pool, h_ready, T * q + t + 1, pool_turn)
                pool.tensor_tensor(xin[:, t, :], xin[:, t, :], hrow[:, t, :], ALU.add).then_inc(res_ready, 1)

            def keep_base(q, t):
                wait_turn(pool, res_ready, T * q + t + 1, pool_turn)
                pool.tensor_tensor(base[:, t, :], xin[:, t, :], b2row[:, :], ALU.add).then_inc(base_ready, 1)

            def largest_w2():
                pool.wait_ge(w2max_ready, 1)
                pool.partition_all_reduce(scol[:, 1:2], scol[:, 0:1], P, LARGEST).then_inc(w2max_all, 1)

            def rows_next(q, beside=None):
                for t in range(T):
                    if beside and t == T - 1:
                        beside()
                    norm_tile(q, t, mv, ln, mv_ready, ln_step)
                    if t >= 1:
                        residual(q, t - 1)
                residual(q, T - 1)

            def indices(g):
                pool.tensor_copy(idx_s[:, :], perm_s[:, bass.ds(T * g, T)]).then_inc(idx_ready, 1)
                pool.tensor_copy(idx_g[:, :], perm_g[:, bass.ds(T * (g + 2), T)]).then_inc(idx_ready, 1)
                wait_turn(pool, idx_ready, 2 * g + 2, pool_turn)

            def rows_move(g, more):
                for t in range(T):
                    wait_turn(pool, fin_ready, T * g + t + 1, pool_turn)
                    pool.indirect_dma_start(out, bass.IndirectOffsetOnAxis(ap=idx_s[:, t:t + 1], axis=0), base[:, t, :],
                                            None, bounds_check=bound, oob_is_err=False).then_inc(rows_out[t], 16)
                    if more >= 1:
                        wait_turn(pool, rows_out[t], 16 * (g + 1), pool_turn)
                        keep_base(g + 1, t)
                    if more >= 2:
                        wait_turn(pool, base_ready, T * (g + 1) + t + 1, pool_turn)
                        gather(g + 2, t, idx_g[:, t:t + 1])

            pool.wait_ge(varp_ready, 1)
            pool.tensor_tensor(vcol[:, 6, :], vcol[:, 5, :], neghalf[:, :], ALU.pow).then_inc(pow_ready, 1)
            pool.wait_ge(perm_ready, 1)
            for t in range(T):
                gather(0, t, perm_g[:, t:t + 1])
            pool.wait_ge(hot_used, NJ // BJ)
            pool.memset(ah[:, :, GW:512], 0.0).then_inc(pads_zero, 1)
            pool.memset(al[:, :, GW:512], 0.0).then_inc(pads_zero, 1)

            def w1_scale_last(i):
                cols = slice(W1W * i, W1W * (i + 1))
                pool.tensor_tensor(wst1[:, 4:KC, cols], wst1[:, 4:KC, cols], spread(s1row[:, cols], [P, 2, W1W], 1),
                                   ALU.mult).then_inc(w1s_pool, 1)

            pool.wait_ge(s1_ready, 1)
            w1_scale_last(0)
            w1_scale_last(1)
            pool.wait_ge(mv_ready, T)
            pool.tensor_scalar(ln[:, :, 2:3], mv[:, :, 1:2], EPS_LN, None, ALU.add).then_inc(ln_step, 4)
            pool.wait_ge(ln_step, 4)
            pool.tensor_tensor(ln[:, :, 0:1], ln[:, :, 2:3], neghalf[:, 0:T].unsqueeze(2), ALU.pow).then_inc(ln_step, 4)
            pool.wait_ge(ln_step, 8)
            pool.tensor_tensor(ln[:, :, 2:3], mv[:, :, 0:1], ln[:, :, 0:1], ALU.mult).then_inc(ln_step, 4)
            pool.wait_ge(ln_step, 12)
            pool.tensor_scalar(ln[:, :, 1:2], ln[:, :, 2:3], -1.0, None, ALU.mult).then_inc(ln_step, 4)
            w1_scale_last(2)
            for t in range(T):
                residual(0, t)
            pool.wait_ge(w1s_dve, W1C)
            pool.wait_ge(w1s_pool, W1C)
            pool.wait_ge(s1col_done, 1)
            pool.wait_ge(in_b2, 16)
            for t in range(T):
                keep_base(0, t)
                pool.wait_ge(base_ready, t + 1)
                gather(1, t, perm_g[:, T + t:T + t + 1])

            rows_next(1, largest_w2)
            indices(0)
            rows_move(0, 2)
            for g in range(1, GROUP_EDGE0):
                rows_next(g + 1)
                indices(g)
                rows_move(g, 2)

            pool.wait_ge(perm_ready, 2)

            def edge_group(e):
                g = e + GROUP_EDGE0
                pool.tensor_copy(idx_e[:, :], src_g[:, bass.ds(T * e, T)]).then_inc(e_idx_ready, 1)
                wait_turn(pool, e_idx_ready, e + 1, pool_turn)
                wait_turn(pool, e_tr_done, KC * e, pool_turn)
                for t in range(T):
                    pool.indirect_dma_start(xedge[:, t, :], None, x, bass.IndirectOffsetOnAxis(ap=idx_e[:, t:t + 1], axis=0),
                                            bounds_check=bound, oob_is_err=False).then_inc(e_rows_in[t], 16)
                rows_next(g + 1)
                indices(g)
                for t in range(T):
                    norm_tile(e, t, mv_e, ln_e, e_mv_ready, e_ln_step)
                rows_move(g, 2)

            edge_group(0)
            with pool.Fori(1, EG) as e:
                edge_group(e)
            with pool.Fori(GROUP_SCAN0, NG - 2) as g:
                rows_next(g + 1)
                indices(g)
                rows_move(g, 2)
            rows_next(NG - 1)
            pool.tensor_copy(idx_s[:, :], perm_s[:, T * (NG - 2):T * (NG - 1)]).then_inc(idx_ready, 1)
            pool.wait_ge(idx_ready, 2 * (NG - 2) + 1)
            rows_move(NG - 2, 1)
            pool.tensor_copy(idx_s[:, :], perm_s[:, T * (NG - 1):T * NG]).then_inc(idx_ready, 1)
            pool.wait_ge(idx_ready, 2 * (NG - 2) + 2)
            rows_move(NG - 1, 0)
            for t in range(T):
                pool.wait_ge(rows_out[t], 16 * NG)

        @block.tensor
        def _(pe):
            pe.wait_ge(const_done, CONSTS)
            pe.wait_ge(hot_ready, 1)
            for j in range(ET):
                mm = pe.matmul(pst[0][:, 0:NJ], hot_p[:, :, j], hot_j[:, :, j], start=(j == 0), stop=(j == ET - 1))
            mm.then_inc(count_done, 1)
            pe.wait_ge(in_vecs, 80)
            for i in range(5):
                mm = pe.transpose(ps2[1][:, 1, MC * i:MC * (i + 1)], vecs[:, i, :], ident[0:MC, 0:MC])
            mm.then_inc(vecs_done, 1)
            pe.wait_ge(rowtot_ready, 1)
            pe.matmul(pst[1][:, 0:1], before[:, :], tab[:, 1, NJ - 1:NJ], start=True, stop=True).then_inc(offset_done, 1)

            def column_norms(c):
                pe.wait_ge(abs_ready, c + 1)
                for i, bank in enumerate((ps2[0][:, 0, :], ps2[0][:, 1, :], ps2[1][:, 0, :])):
                    mm = pe.matmul(bank, ones16[:, :], w1abs[:, c % 2, W1W * i:W1W * (i + 1)],
                                   start=(c == 0), stop=(c == KC - 1))
                mm.then_inc(abs_used, 1)

            for b in range(NJ // BJ):
                pe.wait_ge(hot_ready, b + 2)
                for j in range(BJ):
                    mm = pe.matmul(pst[0][0:R, 128:128 + 2 * NJ], ring_b[:, b % 2, :, j], ring_a[:, b % 2, :, :, j],
                                   start=(b == 0 and j == 0), stop=(b == NJ // BJ - 1 and j == BJ - 1))
                mm.then_inc(hot_used, 1)
                if b < KC:
                    column_norms(b)
            pe.wait_ge(s1_ready, 1)
            for m in range(MC):
                mm = pe.matmul(ps2[1][:, 1, 64 + m:65 + m], s1row[0:1, P * m:P * (m + 1)], ones[0:1, 0:1], start=True, stop=True)
            mm.then_inc(s1col_done, 1)

            def transpose_chunk(q, c):
                if c == 0:
                    wait(pe, h_ready, T * (q + 1))
                wait(pe, xl_ready, KC * q + c - 1)
                for t in range(T):
                    mm = pe.transpose(pst[c % 2][:, R * t:R * (t + 1)], hrow[0:R, t, P * c:P * (c + 1)], ident[0:R, 0:R])
                mm.then_inc(tr_done, 1)

            def edge_chunk(e, q, c):
                if c == 0:
                    wait(pe, e_h_ready, T * (e + 1))
                    wait(pe, xl_ready, KC * (q + 1))
                if c >= 2:
                    wait(pe, e_msg_ready, KC * e + c - 1)
                for t in range(T):
                    mm = pe.transpose(pst[c % 2][:, R * t:R * (t + 1)], xedge[0:R, t, P * c:P * (c + 1)], ident[0:R, 0:R])
                mm.then_inc(e_tr_done, 1)

            def first_product(g, beside=None):
                wait(pe, xl_ready, KC * (g + 1))
                for m in range(MC):
                    wait(pe, al_ready, MC * g + m - 1)
                    if isinstance(g, int) and g == 0:
                        pe.wait_ge(w1l_ready, P * m // W1W + 1)
                    col = slice(P * m, P * (m + 1))
                    for k in range(KC):
                        pe.matmul(ps1[m % 2][:, 0:GW], w1h[:, k, col], xth[:, k, :], start=(k == 0), stop=False)
                        pe.matmul(ps1[m % 2][:, 0:GW], w1h[:, k, col], xtl[:, k, :], start=False, stop=False)
                        mm = pe.matmul(ps1[m % 2][:, 0:GW], w1l[:, k, col], xth[:, k, :], start=False, stop=(k == KC - 1))
                    mm.then_inc(mm1_done, 1)
                    if beside:
                        beside(m)

            def second_product(g, t, half):
                o = ps2[t % 2]
                if half == 0:
                    wait(pe, fin_ready, T * g + t - 1)
                for m in range(MC // 2 * half, MC // 2 * (half + 1)):
                    if t == 0:
                        wait(pe, al_ready, MC * g + m + 1)
                    if isinstance(g, int) and g == 0 and t == 0:
                        pe.wait_ge(w2l_ready, m + 1)
                    rows_h, rows_l = ah[:, m, R * t:R * t + P], al[:, m, R * t:R * t + P]
                    lo, hi = slice(0, HALF), slice(HALF, D)
                    s, e = m == 0, m == MC - 1
                    pe.matmul(o[:, 0, 0:HALF], rows_h, w2h[:, m, lo], start=s, stop=False)
                    pe.matmul(o[:, 1, 0:HALF], rows_h, w2h[:, m, hi], start=s, stop=False)
                    pe.matmul(o[:, 0, 0:HALF], rows_h, w2l[:, m, lo], start=False, stop=False)
                    pe.matmul(o[:, 1, 0:HALF], rows_h, w2l[:, m, hi], start=False, stop=False)
                    pe.matmul(o[:, 0, 0:HALF], rows_l, w2h[:, m, lo], start=False, stop=e)
                    mm = pe.matmul(o[:, 1, 0:HALF], rows_l, w2h[:, m, hi], start=False, stop=e)
                if half == 1:
                    mm.then_inc(mm2_done, 1)

            def group(g, nxt=True, edges=None, beside=None, picks=None):
                first_product(g, beside)
                if edges is not None:
                    wait(pe, e_msg_ready, KC * edges)
                if beside:
                    pe.wait_ge(row_used, ET // T)
                for slot in range(2 * T):
                    if nxt and slot < 3:
                        transpose_chunk(g + 1, 2 * slot)
                        transpose_chunk(g + 1, 2 * slot + 1)
                    if edges is not None and 4 <= slot < 7:
                        edge_chunk(edges, g + 1, 2 * (slot - 4))
                        edge_chunk(edges, g + 1, 2 * (slot - 4) + 1)
                    if picks and slot == 5:
                        picks()
                    second_product(g, slot // 2, slot % 2)

            def sort_edges():
                pe.wait_ge(sort_hot, 1)
                pe.wait_ge(xl_ready, KC * GROUP_EDGE0)
                for j in range(ET):
                    mm = pe.matmul(pst[0][0:R, 0:2 * ET], slot_hot[:, j, :], tile_hot[:, j, :, :].rearrange("p s a -> p (s a)"),
                                   start=(j == 0), stop=(j == ET - 1))
                mm.then_inc(sorted_done, 1)

            def dst_rows(m):
                i = m - 5
                if not 0 <= i < ET // T:
                    return
                if i == 0:
                    pe.wait_ge(diag_ready, 1)
                wait(pe, row_used, i - 1)
                pe.matmul(pst[i % 2][:, 0:GW], ones[0:R, :], dst_diag[:, T * i:T * (i + 1), :].rearrange("p a b -> p (a b)"),
                          start=True, stop=True).then_inc(row_done, 1)

            def pick_free():
                pe.wait_ge(pick_hot, 1)
                pe.wait_ge(xl_ready, KC * (GROUP_EDGE0 + 1))
                for i in range(ET):
                    sl = slice(R * i, R * (i + 1))
                    pe.matmul(pst[0][0:R, ET * i:ET * (i + 1)], s2[0:R, sl], perm_f[0:R, FREE_T:NT], start=True, stop=True)
                    pe.matmul(pst[0][0:R, 400 + i:401 + i], s0[0:1, sl], ones[0:1, 0:1], start=True, stop=True)
                    mm = pe.matmul(pst[0][0:R, 420 + i:421 + i], first[0:1, 1 + R * i:1 + R * (i + 1)], ones16[0:1, 0:1],
                                   start=True, stop=True)
                mm.then_inc(picks_done, 1)

            for c in range(KC):
                transpose_chunk(0, c)
            pe.wait_ge(pads_zero, 2)
            group(0)
            group(1)
            sort_edges()
            group(2, beside=dst_rows, picks=pick_free)
            pe.wait_ge(picks_copied, 1)
            group(GROUP_EDGE0, edges=0)
            with pe.Fori(1, EG) as e:
                group(e + GROUP_EDGE0, edges=e)
            pe.wait_ge(e_msg_ready, KC * EG)
            with pe.Fori(GROUP_SCAN0, NG - 1) as g:
                group(g)
            group(NG - 1, nxt=False)

        @block.scalar
        def _(act):
            for c in range(KC):
                act.wait_ge(in_w1[c], 16)
                wait(act, abs_used, c - 1)
                act.activation(w1abs[:, c % 2, :], wst1[:, c, :], ACT.Abs).then_inc(abs_ready, 1)

            def w1_high(i):
                cols = slice(W1W * i, W1W * (i + 1))
                act.wait_ge(w1s_dve, i + 1)
                act.wait_ge(w1s_pool, i + 1)
                act.activation(w1h[:, :, cols], wst1[:, :, cols], ACT.Copy).then_inc(w1h_ready, 1)

            def norm_rows(q, t):
                first_group = isinstance(q, int) and q == 0
                wait(act, ln_step, 4 * T if first_group else 4 * (T * q + t + 1))
                wait(act, tr_done, KC * q)
                wait(act, res_ready, T * (q - 1) + t + 1)
                act.activation(hrow[:, t, :], xin[:, t, :], ACT.Relu, scale=ln[:, t, 0:1], bias=ln[:, t, 1:2]).then_inc(h_ready, 1)

            def edge_norm_rows(e):
                for t in range(T):
                    wait(act, e_ln_step, 4 * (T * e + t + 1))
                    act.activation(xedge[:, t, :], xedge[:, t, :], ACT.Relu, scale=ln_e[:, t, 0:1],
                                   bias=ln_e[:, t, 1:2]).then_inc(e_h_ready, 1)

            def x_high(q, c, tail):
                wait(act, sum_done if tail else tr_done, KC * (q - TAIL) + c + 1 if tail else KC * q + c + 1)
                source = xsum[:, c % 2, :] if tail else pst[c % 2][:, 0:GW]
                act.activation(xth[:, c, :], source, ACT.Copy, scale=XS).then_inc(xh_ready, 1)

            def hidden(g, m):
                wait(act, mm1_done, MC * g + m + 1)
                act.activation(ps1[m % 2][:, 0:GW], ps1[m % 2][:, 0:GW], ACT.Relu, scale=vcol[:, 13, m:m + 1],
                               bias=vcol[:, 14, m:m + 1]).then_inc(act_done, 1)
                wait(act, act_done, MC * g + m + 1)
                act.activation(ah[:, m, 0:GW], ps1[m % 2][:, 0:GW], ACT.Copy).then_inc(ah_ready, 1)

            def w2_high(m):
                act.activation(w2h[:, m, :], wst2[:, m, :], ACT.Copy, scale=vcol[:, 15, m:m + 1]).then_inc(w2h_ready, 1)

            w1_high(0)
            w1_high(1)
            for t in range(T):
                norm_rows(0, t)
            for c in range(KC):
                x_high(0, c, False)
            w1_high(2)
            act.wait_ge(bn_ready, 1)

            def group(g, tail=False, nxt=True, edges=None, scan=None):
                for m in range(MC):
                    hidden(g, m)
                    if nxt and m in (3, 5, 7, 9):
                        norm_rows(g + 1, (m - 3) // 2)
                    if isinstance(g, int) and g == 0 and m == 8:
                        act.wait_ge(w2scale_ready, 1)
                    if isinstance(g, int) and g == 0 and m >= 8:
                        for i in range(3 * (m - 8), 3 * (m - 7)):
                            w2_high(i)
                if scan is not None:
                    wait(act, msg_in, 16 * (scan + 1))
                    act.activation(s1, s0, ACT.Copy, scale=tcol[:, 0:1]).then_inc(scan_act, 1)
                for c in range(KC if nxt else 0):
                    if edges is not None and c == 4:
                        edge_norm_rows(edges)
                    if scan is not None and c == 4:
                        wait(act, scan_step, SCAN_STEPS * scan + 3)
                        act.activation(s1, s1, ACT.Exp).then_inc(scan_act, 1)
                    x_high(g + 1, c, tail)

            group(0)
            act.wait_ge(in_t, 16)
            group(1)
            group(2)
            group(GROUP_EDGE0, edges=0)
            with act.Fori(1, EG) as e:
                group(e + GROUP_EDGE0, edges=e)
            group(GROUP_SCAN0, scan=0)
            with act.Fori(1, KC) as c:
                group(c + GROUP_SCAN0, scan=c)
            with act.Fori(TAIL - 1, NG - 1) as g:
                group(g, tail=True)
            group(NG - 1, nxt=False)

        @block.vector
        def _(dve):
            step = [0]

            def link(ins):
                step[0] += 1
                ins.then_inc(dve_step, 1)
                dve.wait_ge(dve_step, step[0])

            def power_of_two(ap):
                bits = ap.bitcast(i32)
                link(dve.tensor_scalar(bits, bits, EXP_BITS, EXP_BITS, ALU.bitwise_and, ALU.bitwise_xor))
                link(dve.tensor_scalar(ap, ap, 8192.0, None, ALU.mult))

            def divmod_rows(q_i, q_f, r, value):
                link(dve.tensor_scalar(q_i, value, 62.0, 1.0 / R, ALU.subtract, ALU.mult))
                link(dve.tensor_copy(q_f, q_i))
                link(dve.scalar_tensor_tensor(r, q_f, -float(R), value, ALU.mult, ALU.add))

            dve.wait_ge(const_done, CONSTS)
            dve.wait_ge(in_edges, 32)
            e_in, e_out = edge_i[0:R, :, :], edge_f[0:R, :, :]
            link(dve.tensor_scalar(e_in[:, 2, :], e_in[:, 1, :], 7, None, ALU.logical_shift_right))
            link(dve.tensor_scalar(e_in[:, 3, :], e_in[:, 1, :], 127, None, ALU.bitwise_and))
            dve.tensor_copy(e_out, e_in)
            link(dve.tensor_copy(edge16[0:R, :, :], e_in[:, 2:4, :]))
            dve.tensor_tensor(hot_p, lane16[0:R, :, :], spread(edge16[0:R, 1, :], [R, P, ET], 1), ALU.is_equal)
            dve.tensor_tensor(hot_j, lane16[0:R, 0:NJ, :], spread(edge16[0:R, 0, :], [R, NJ, ET], 1),
                              ALU.is_equal).then_inc(hot_ready, 1)
            valid, rank_in, free, far, rank, q_f, rb = (tab[:, i, :] for i in range(7))
            link(dve.tensor_scalar(valid, node[:, :], float(N), None, ALU.is_lt))
            dve.wait_ge(vecs_done, 1)
            link(dve.tensor_copy(vcol[:, 0:5, :], ps2[1][:, 1, 0:5 * MC].rearrange("p (i m) -> p i m", i=5)))
            vb1, vgamma, vbeta, vmean, vvar, v_eps, v_rsqrt, v_inv, v_bias, v_s1, v_unscale, v_bound, v_ca, v_scale, v_shift, v_w2 = \
                (vcol[:, i, :] for i in range(16))
            dve.tensor_scalar(v_eps, vvar, EPS_BN, None, ALU.add).then_inc(varp_ready, 1)
            dve.wait_ge(count_done, 1)
            link(dve.scalar_tensor_tensor(free, pst[0][:, 0:NJ], 0.0, valid, ALU.is_equal, ALU.mult))
            dve.tensor_tensor_scan(rank_in, ones[:, 0:NJ], free, 0.0, ALU.mult, ALU.add).then_inc(rowtot_ready, 1)
            dve.wait_ge(rowtot_ready, 1)
            link(dve.tensor_scalar(far, free, -float(NOWHERE), float(NOWHERE) - 1.0, ALU.mult, ALU.add))
            dve.wait_ge(offset_done, 1)
            link(dve.tensor_copy(scol[:, 6:7], pst[1][:, 0:1]))
            link(dve.scalar_tensor_tensor(rank, rank_in, scol[:, 6:7], far, ALU.add, ALU.add))
            divmod_rows(tab_i[:, :], q_f, rb, rank)
            dve.tensor_copy(rank16[:, 0, :], q_f)
            link(dve.tensor_copy(rank16[:, 1, :], rb))
            for b in range(NJ // BJ):
                js = slice(BJ * b, BJ * (b + 1))
                wait(dve, hot_used, b - 1)
                dve.tensor_tensor(ring_b[:, b % 2, :, :], lane16[:, 0:R, 0:BJ], spread(rank16[:, 1, js], [P, R, BJ], 1), ALU.is_equal)
                wait(dve, hot_ready, b + 1)
                link(dve.tensor_tensor(tile_of, lane16[:, 0:NJ, 0:BJ], spread(rank16[:, 0, js], [P, NJ, BJ], 1), ALU.is_equal))
                dve.tensor_scalar(ring_a[:, b % 2, 0, :, :], tile_of, part0[:, 0:1], None, ALU.mult)
                dve.tensor_tensor(ring_a[:, b % 2, 1, :, :], tile_of, spread(column16[:, js], [P, NJ, BJ], 1),
                                  ALU.mult).then_inc(hot_ready, 1)
            dve.wait_ge(hot_used, NJ // BJ)
            link(dve.tensor_copy(perm2[0:R, :, :], pst[0][0:R, 128:128 + 2 * NJ].rearrange("p (k a) -> p k a", k=2)))
            link(dve.scalar_tensor_tensor(perm_f[0:R, :], perm2[0:R, 1, :], float(P), perm2[0:R, 0, :], ALU.mult, ALU.add))
            dve.tensor_copy(perm_g[0:R, 0:FREE_T], perm_f[0:R, 0:FREE_T])
            dve.tensor_copy(perm_s[0:R, 0:FREE_T], perm_f[0:R, 0:FREE_T]).then_inc(perm_ready, 1)

            dve.wait_ge(abs_used, KC)
            for i, bank in enumerate((ps2[0][:, 0, :], ps2[0][:, 1, :], ps2[1][:, 0, :])):
                last = dve.tensor_scalar(s1row[:, 512 * i:512 * (i + 1)], bank, 1e-30, None, ALU.max)
            link(last)
            bits = s1row.bitcast(i32)
            link(dve.tensor_scalar(bits, bits, EXP_BITS, EXP_BITS, ALU.bitwise_and, ALU.bitwise_xor))
            dve.tensor_scalar(s1row, s1row, 8192.0, None, ALU.mult).then_inc(s1_ready, 1)
            dve.wait_ge(s1_ready, 1)

            def w1_scale(i):
                cols = slice(W1W * i, W1W * (i + 1))
                dve.tensor_tensor(wst1[:, 0:4, cols], wst1[:, 0:4, cols], spread(s1row[:, cols], [P, 4, W1W], 1),
                                  ALU.mult).then_inc(w1s_dve, 1)

            def w1_low(i):
                cols = slice(W1W * i, W1W * (i + 1))
                dve.wait_ge(w1h_ready, i + 1)
                dve.tensor_tensor(w1l[:, :, cols], wst1[:, :, cols], w1h[:, :, cols], ALU.subtract).then_inc(w1l_ready, 1)

            w1_scale(0)

            def statistics(q, t, source, raw, m, s_in, s_raw, s_mv):
                wait(dve, s_in[t], 16 * (q + 1))
                dve.bn_stats(raw[:, t, 0:6], source[:, t, 0:HALF])
                dve.bn_stats(raw[:, t, 6:12], source[:, t, HALF:D]).then_inc(s_raw, 1)
                wait_turn(dve, s_raw, T * q + t + 1, dve_turn)
                dve.bn_aggr(m[:, t, :], raw[:, t, :]).then_inc(s_mv, 1)

            for t in range(T):
                statistics(0, t, xin, bnraw, mv, rows_in, bn_raw, mv_ready)
            w1_low(0)
            w1_scale(1)
            w1_scale(2)

            dve.wait_ge(s1col_done, 1)
            link(dve.tensor_tensor(v_bias, vb1, vmean, ALU.subtract))
            link(dve.tensor_copy(v_s1, ps2[1][:, 1, 64:64 + MC]))
            link(dve.reciprocal(v_unscale, v_s1))
            dve.wait_ge(pow_ready, 1)
            link(dve.tensor_tensor(v_inv, v_rsqrt, vgamma, ALU.mult))
            link(dve.tensor_tensor(v_bias, v_bias, v_inv, ALU.mult))
            link(dve.tensor_tensor(v_bias, v_bias, vbeta, ALU.add))
            link(dve.scalar_tensor_tensor(v_bound, v_inv, -1.0, v_inv, ALU.mult, ALU.max))
            link(dve.scalar_tensor_tensor(v_bound, v_bound, 1.02 * XMAX * 2.0 ** 15, v_unscale, ALU.mult, ALU.mult))
            link(dve.scalar_tensor_tensor(v_ca, v_bias, -1.0, v_bias, ALU.mult, ALU.max))
            link(dve.tensor_scalar(v_bound, v_bound, 1e-30, None, ALU.max))
            link(dve.tensor_tensor(v_ca, v_ca, v_bound, ALU.add))
            power_of_two(v_ca)
            link(dve.tensor_tensor(v_scale, v_inv, v_ca, ALU.mult))
            link(dve.scalar_tensor_tensor(v_scale, v_scale, 1.0 / XS, v_unscale, ALU.mult, ALU.mult))
            link(dve.tensor_tensor(v_shift, v_bias, v_ca, ALU.mult))
            dve.reciprocal(v_bound, v_ca).then_inc(bn_ready, 1)

            w1_low(1)

            def x_sum(q, c):
                wait(dve, tr_done, KC * q + c + 1)
                wait(dve, agg_back, 16 * (q - TAIL + 1))
                dve.tensor_tensor(xsum[:, c % 2, :], pst[c % 2][:, 0:GW], agg_in[:, c, :], ALU.add).then_inc(sum_done, 1)

            def x_low(q, c, tail=False):
                wait(dve, xh_ready, KC * q + c + 1)
                source = xsum[:, c % 2, :] if tail else pst[c % 2][:, 0:GW]
                dve.scalar_tensor_tensor(xtl[:, c, :], source, XS, xth[:, c, :], ALU.mult, ALU.subtract).then_inc(xl_ready, 1)

            def hidden_low(g, m):
                wait(dve, ah_ready, MC * g + m + 1)
                dve.tensor_tensor(al[:, m, 0:GW], ps1[m % 2][:, 0:GW], ah[:, m, 0:GW], ALU.subtract).then_inc(al_ready, 1)

            def finish(g, t):
                wait(dve, base_ready, T * g + t + 1)
                wait(dve, mm2_done, T * g + t + 1)
                rows2 = base[:, t, :].rearrange("p (h n) -> p h n", h=2)
                dve.scalar_tensor_tensor(rows2, ps2[t % 2][:, :, 0:HALF], scol[:, 3:4], rows2, ALU.mult, ALU.add).then_inc(fin_ready, 1)

            def w2_max(q):
                dve.wait_ge(in_w2[q], 16)
                link(dve.tensor_reduce(pcol[:, 0, 4 * q:4 * q + 4], wst2[:, 4 * q:4 * q + 4, :], AX.X, ALU.max, apply_absolute_value=True))

            def w2_max_rows():
                link(dve.tensor_tensor(pcol[:, 1, :], pcol[:, 0, :], v_bound, ALU.mult))
                dve.tensor_reduce(scol[:, 0:1], pcol[:, 1, :], AX.X, ALU.max).then_inc(w2max_ready, 1)

            def w2_scale():
                dve.wait_ge(w2max_all, 1)
                link(dve.tensor_scalar(scol[:, 2:3], scol[:, 1:2], 1e-30, None, ALU.max))
                power_of_two(scol[:, 2:3])
                link(dve.reciprocal(scol[:, 3:4], scol[:, 2:3]))
                dve.tensor_scalar(v_w2, v_bound, scol[:, 2:3], None, ALU.mult).then_inc(w2scale_ready, 1)
                dve.wait_ge(w2scale_ready, 1)

            def w2_low(m):
                dve.wait_ge(w2h_ready, m + 1)
                dve.scalar_tensor_tensor(w2l[:, m, :], wst2[:, m, :], v_w2[:, m:m + 1], w2h[:, m, :],
                                         ALU.mult, ALU.subtract).then_inc(w2l_ready, 1)

            sor_src, sor_dst = sorted_e[0:R, 0, :], sorted_e[0:R, 1, :]

            def count_setup():
                dve.wait_ge(in_dstrow, 16)
                dve.memset(count3[:, :, :], 0.0)
                link(dve.tensor_copy(dst_cols, s0[0:R, :].bitcast(i32).rearrange("p (q j) -> p j q", j=ET)))
                link(dve.tensor_tensor(dst_tied, dst_cols, spread(tie[0:R, 0:R], [R, ET, R], 1), ALU.add))

            def count(j):
                mine = edge_f[0:R, 1, j:j + 1]
                junk = s0[0:R, :].rearrange("p (j q) -> p j q", j=ET)
                if j > 0:
                    link(dve.tensor_scalar(junk[:, 0:j, :], dst_cols[:, 0:j, :], mine, 0.0, ALU.is_le, ALU.add,
                                      accum_out=count3[0:R, 0, j:j + 1]))
                if j < ET - 1:
                    link(dve.tensor_scalar(junk[:, j + 1:ET, :], dst_cols[:, j + 1:ET, :], mine, 0.0, ALU.is_lt, ALU.add,
                                      accum_out=count3[0:R, 1, j:j + 1]))
                link(dve.tensor_scalar(junk[:, j, :], dst_tied[:, j, :], mine, 0.0, ALU.is_lt, ALU.add,
                                  accum_out=count3[0:R, 2, j:j + 1]))

            def place_edges():
                a, b, c = (count3[0:R, i, :] for i in range(3))
                link(dve.tensor_tensor(a, a, b, ALU.add))
                link(dve.tensor_tensor(a, a, c, ALU.add))
                divmod_rows(edge_i[0:R, 2, :], b, c, a)
                link(dve.tensor_tensor(slot_hot, spread(lane[0:R, 0:R], [R, ET, R], 1), spread(c, [R, ET, R], 2), ALU.is_equal))
                link(dve.tensor_tensor(tile_eq, spread(lane[0:R, 0:ET], [R, ET, ET], 1), spread(b, [R, ET, ET], 2), ALU.is_equal))
                for i in range(2):
                    last = dve.tensor_tensor(tile_hot[:, :, i, :], tile_eq, spread(edge_f[0:R, i, :], [R, ET, ET], 2), ALU.mult)
                last.then_inc(sort_hot, 1)

            def spread_dst():
                dve.wait_ge(sorted_done, 1)
                link(dve.tensor_copy(sorted_e[0:R, :, :], pst[0][0:R, 0:2 * ET].rearrange("p (s a) -> p s a", s=2)))
                link(dve.tensor_copy(src_g[0:R, :], sor_src))
                dve.tensor_tensor(dst_diag, spread(ident[0:R, 0:R], [R, ET, R], 1), spread(sor_dst, [R, ET, R], 2),
                                  ALU.mult).then_inc(diag_ready, 1)

            def keep_dst_row(i):
                dve.wait_ge(row_done, i + 1)
                dve.tensor_copy(s0[:, GW * i:GW * (i + 1)], pst[i % 2][:, 0:GW]).then_inc(row_used, 1)

            def mark_segments():
                dve.wait_ge(row_used, ET // T)
                dve.memset(first[:, 0:1], 1.0)
                dve.memset(first[:, E:E + 1], 1.0)
                link(dve.tensor_tensor(first[:, 1:E], s0[:, 1:E], s0[:, 0:E - 1], ALU.not_equal))
                dve.tensor_scalar(cut[:, 0:E + 1], first[:, 0:E + 1], -3e38, None, ALU.mult)
                link(dve.tensor_scalar(keep[:, 0:E + 1], first[:, 0:E + 1], -1.0, 1.0, ALU.mult, ALU.add))

            def rank_not_last():
                link(dve.tensor_tensor_scan(s1, keep[:, 1:E + 1], keep[:, 1:E + 1], 0.0, ALU.add, ALU.max))

            def pick_one_hots():
                q_int = s2.bitcast(i32)
                link(dve.tensor_scalar(q_int, s1, 63.0, 1.0 / R, ALU.subtract, ALU.mult))
                link(dve.tensor_copy(s0, q_int))
                link(dve.scalar_tensor_tensor(s1, s0, -float(R), s1, ALU.mult, ALU.add))
                dve.tensor_scalar(s2, s1, part1[:, 0:1], None, ALU.is_equal).then_inc(pick_hot, 1)

            def place_tail():
                dve.wait_ge(picks_done, 1)
                dve.tensor_copy(picks, pst[0][0:R, 0:440]).then_inc(picks_copied, 1)
                dve.wait_ge(picks_copied, 1)
                cube = lambda i: s1[0:R, 500 * i:500 * i + ET * ET].rearrange("p (i a) -> p i a", i=ET)
                col = lambda i: s1[0:R, 1500 + ET * i:1500 + ET * (i + 1)]
                link(dve.tensor_tensor(cube(1), spread(lane[0:R, 0:ET], [R, ET, ET], 1), spread(picks[:, 400:420], [R, ET, ET], 2),
                                       ALU.is_equal))
                link(dve.tensor_tensor(cube(2), cube(1), picks[:, 0:400].rearrange("p (i a) -> p i a", i=ET), ALU.mult))
                link(dve.tensor_reduce(col(0), cube(2), AX.X, ALU.add))
                link(dve.tensor_tensor(col(1), sor_dst, col(0), ALU.subtract))
                link(dve.tensor_tensor(col(1), col(1), picks[:, 420:440], ALU.mult))
                link(dve.tensor_tensor(col(2), col(1), col(0), ALU.add))
                dve.tensor_copy(perm_g[0:R, FREE_T:NT], col(2))
                dve.tensor_copy(perm_s[0:R, FREE_T:NT], col(2)).then_inc(perm_ready, 1)

            def edge_message(e, c):
                wait(dve, e_tr_done, KC * e + c + 1)
                wait(dve, e_msg_out[c % 2], 16 * (KC // 2 * e + c // 2))
                dve.tensor_scalar(emsg[:, c % 2, :], pst[c % 2][:, 0:GW], EPS_MSG, None, ALU.add).then_inc(e_msg_ready, 1)

            def scan(c, at, ins):
                ins.then_inc(scan_step, 1)
                wait(dve, scan_step, SCAN_STEPS * c + at)

            def scan_max(c):
                wait(dve, scan_act, 2 * c + 1)
                scan(c, 1, dve.tensor_tensor_scan(s2, cut[:, 0:E], s1, 0.0, ALU.add, ALU.max))
                scan(c, 2, dve.tensor_tensor_scan(s2[:, ::-1], cut[:, 1:E + 1][:, ::-1], s2[:, ::-1], 0.0, ALU.add, ALU.max))

            def scan_shift(c):
                scan(c, 3, dve.tensor_tensor(s1, s1, s2, ALU.subtract))

            def scan_sums(c):
                wait(dve, scan_act, 2 * c + 2)
                scan(c, 4, dve.tensor_tensor(s0, s0, s1, ALU.mult))
                scan(c, 5, dve.tensor_tensor_scan(s2, keep[:, 0:E], s1, 0.0, ALU.mult, ALU.add))
                scan(c, 6, dve.tensor_tensor_scan(s1, keep[:, 0:E], s0, 0.0, ALU.mult, ALU.add))
                scan(c, 7, dve.tensor_scalar(s2, s2, EPS_SUM, None, ALU.add))

            def scan_reciprocal(c, parts):
                for i in parts:
                    ins = dve.reciprocal(s2[:, GW * i:GW * (i + 1)], s2[:, GW * i:GW * (i + 1)])
                return ins

            def scan_quotient(c, ins):
                scan(c, 8, ins)
                scan(c, 9, dve.tensor_tensor(s1, s1, s2, ALU.mult))
                scan(c, 10, dve.tensor_tensor(s1, s1, first[:, 1:E + 1], ALU.mult))

            def group(g, tail=False, nxt=True, edges=None, scans=None, sort=None):
                for m in range(MC):
                    hidden_low(g, m)
                    if nxt and m in (2, 4, 6, 8):
                        statistics(g + 1, (m - 2) // 2, xin, bnraw, mv, rows_in, bn_raw, mv_ready)
                    if sort == 2:
                        if m == 1:
                            spread_dst()
                        if 6 <= m < 6 + ET // T:
                            keep_dst_row(m - 6)
                    if sort == 0:
                        if 5 <= m < 8:
                            w2_max(m - 5)
                        if m == 7:
                            w2_max_rows()
                        if m == 8:
                            w2_scale()
                        if m >= 9:
                            for i in range(3 * (m - 9), 3 * (m - 8)):
                                w2_low(i)
                if sort == 0:
                    for i in range(9, MC):
                        w2_low(i)

                def low(*chunks):
                    for c in chunks if nxt else ():
                        if tail and c % 2 == 0:
                            x_sum(g + 1, c)
                            x_sum(g + 1, c + 1)
                        x_low(g + 1, c, tail)

                def counts(lo, hi):
                    for j in range(lo, hi):
                        count(j)

                low(0, 1)
                if edges is not None:
                    for t in range(T):
                        statistics(edges, t, xedge, bnraw_e, mv_e, e_rows_in, e_bn_raw, e_mv_ready)
                if scans is not None:
                    scan_max(scans)
                if sort == 1:
                    counts(9, 12)
                if sort == 2:
                    mark_segments()
                low(2, 3)
                if scans is not None:
                    scan_shift(scans)
                if sort == 0:
                    count_setup()
                if sort == 1:
                    counts(12, 13)
                if sort == 2:
                    rank_not_last()
                finish(g, 0)
                low(4, 5)
                if scans is not None:
                    scan_sums(scans)
                if sort == 0:
                    counts(0, 3)
                if sort == 1:
                    counts(13, 16)
                if sort == 2:
                    pick_one_hots()
                finish(g, 1)
                if edges is not None:
                    for c in range(4):
                        edge_message(edges, c)
                if scans is not None:
                    scan_reciprocal(scans, range(0, 3))
                if sort == 0:
                    counts(3, 6)
                if sort == 1:
                    counts(16, ET)
                finish(g, 2)
                if edges is not None:
                    for c in range(4, KC):
                        edge_message(edges, c)
                if scans is not None:
                    scan_quotient(scans, scan_reciprocal(scans, range(3, 5)))
                if sort == 0:
                    counts(6, 9)
                if sort == 1:
                    place_edges()
                if sort == 2:
                    place_tail()
                finish(g, 3)

            for c in range(KC):
                x_low(0, c)
            w1_low(2)
            group(0, sort=0)
            group(1, sort=1)
            group(2, sort=2)
            group(GROUP_EDGE0, edges=0)
            with dve.Fori(1, EG) as e:
                group(e + GROUP_EDGE0, edges=e)
            group(GROUP_SCAN0, scans=0)
            with dve.Fori(1, KC) as c:
                group(c + GROUP_SCAN0, scans=c)
            with dve.Fori(TAIL - 1, NG - 1) as g:
                group(g, tail=True)
            group(NG - 1, nxt=False)


_INS = ["x", "src", "dst", "L0_gnn_t", "L0_gnn_W1", "L0_gnn_b1", "L0_gnn_bn_gamma", "L0_gnn_bn_beta", "L0_gnn_bn_mean",
        "L0_gnn_bn_var", "L0_gnn_W2", "L0_gnn_b2"]


def kernel(**inputs):
    import numpy as np
    import concourse.bacc as bacc
    from concourse.bass_utils import run_bass_kernel_spmd

    nc = bacc.Bacc("TRN2", target_bir_lowering=False, num_devices=1)
    arrays, args = {}, []
    for name in _INS:
        a = np.ascontiguousarray(inputs[name])
        if a.ndim == 0:
            a = a.reshape(1)
        arrays[name + "_dram"] = a
        args.append(nc.dram_tensor(name + "_dram", a.shape, mybir.dt.from_np(a.dtype), kind="ExternalInput").ap())
    out = nc.dram_tensor("out_dram", inputs["x"].shape, mybir.dt.float32, kind="ExternalOutput").ap()
    gnn_layer(nc, *args, out)
    r = run_bass_kernel_spmd(nc, [arrays], core_ids=[0])
    return r.results[0]["out_dram"]
```
